# Optimizing a Trainium2 kernel written in Bass

```python
import numpy as np
import jax
import jax.numpy as jnp

def _softmax(x, axis=-1):
    return jax.nn.softmax(x, axis=axis)

def _gelu(x):
    return jax.nn.gelu(x, approximate=True)

def _silu(x):
    return jax.nn.silu(x)

def _sigmoid(x):
    return jax.nn.sigmoid(x)

def _layernorm(x, axis=-1, eps=1e-05):
    m = jnp.mean(x, axis=axis, keepdims=True)
    v = jnp.var(x, axis=axis, keepdims=True)
    return (x - m) / jnp.sqrt(v + eps)

def _scatter_add(tgt, idx, src, axis=0):
    return tgt.at[idx].add(src)

def _segment_sum(src, seg, n):
    return jax.ops.segment_sum(src, seg, n)
kernel_name = 'mk_metaformer_d1_conv_nchw512_r4_369be5'

def setup_inputs(seed: int=0):
    np.random.seed(seed)
    _w = jnp.asarray

    def _rec_inputs():
        import jax
        import jax.numpy as jnp
        _gk = jax.random.key(seed)
        x = -0.000125 + 0.9999 * jax.random.normal(jax.random.fold_in(_gk, 1), (16, 128, 16, 16), jnp.float32)
        return x
    x = _rec_inputs()

    def _L0_conv_setup():
        import jax, jax.numpy as jnp
        import numpy as np
        EPS = 1e-08

        def _compute_W(V, C, eps=EPS):
            W = jnp.eye(C, dtype=V.dtype)

            def step(W, v):
                v = v / (jnp.linalg.norm(v) + eps)
                W = W - 2.0 * jnp.outer(v, v @ W)
                return (W, None)
            W, _ = jax.lax.scan(step, W, V)
            return W
        key = jax.random.key(seed)
        k1, k2 = jax.random.split(key)
        x = jax.random.normal(k1, (16, 128, 16, 16), dtype=jnp.float32)
        V = jax.random.normal(k2, (32, 128), dtype=jnp.float32)
        return {'x': x, 'V': V}
    _L0_conv_all = _L0_conv_setup()
    _L0_conv_in = {k: v for k, v in _L0_conv_all.items() if k in ('V',)}
    del _L0_conv_all

    def _L0_ffn_setup():
        import jax, jax.numpy as jnp
        import numpy as np
        NUM_EXPERTS = 32
        GROUP_SIZE = 4
        NUM_GROUPS = NUM_EXPERTS // GROUP_SIZE
        C_CAP = 1.0
        key = jax.random.key(seed)
        ks = jax.random.split(key, 5)
        B, S, H = (16, 512, 128)
        D_FF = int(H * 4 * (2.0 / 3.0))
        x = jax.random.normal(ks[0], (B, S, H), dtype=jnp.float32)
        W_router = jax.random.normal(ks[1], (H, NUM_EXPERTS), dtype=jnp.float32) * (1.0 / np.sqrt(H))
        b_router = jnp.zeros((NUM_EXPERTS,), dtype=jnp.float32)
        W_up = jax.random.normal(ks[2], (NUM_GROUPS, H, D_FF), dtype=jnp.float32) * (1.0 / np.sqrt(H))
        b_up = jnp.zeros((NUM_GROUPS, D_FF), dtype=jnp.float32)
        W_down = jax.random.normal(ks[3], (NUM_EXPERTS, D_FF, H), dtype=jnp.float32) * (1.0 / np.sqrt(D_FF))
        b_down = jnp.zeros((NUM_EXPERTS, H), dtype=jnp.float32)
        return {'x': x, 'W_router': W_router, 'b_router': b_router, 'W_up': W_up, 'b_up': b_up, 'W_down': W_down, 'b_down': b_down}
    _L0_ffn_all = _L0_ffn_setup()
    _L0_ffn_in = {k: v for k, v in _L0_ffn_all.items() if k in ('W_router', 'b_router', 'W_up', 'b_up', 'W_down', 'b_down')}
    del _L0_ffn_all
    return {'x': x, 'L0_conv_V': _L0_conv_in['V'], 'L0_ffn_W_router': _L0_ffn_in['W_router'], 'L0_ffn_b_router': _L0_ffn_in['b_router'], 'L0_ffn_W_up': _L0_ffn_in['W_up'], 'L0_ffn_b_up': _L0_ffn_in['b_up'], 'L0_ffn_W_down': _L0_ffn_in['W_down'], 'L0_ffn_b_down': _L0_ffn_in['b_down']}

def reference(x, L0_conv_V, L0_ffn_W_router, L0_ffn_b_router, L0_ffn_W_up, L0_ffn_b_up, L0_ffn_W_down, L0_ffn_b_down):
    import jax
    import jax.numpy as jnp

    def _L0_conv_ref(x, V):
        import jax, jax.numpy as jnp
        import numpy as np
        EPS = 1e-08

        def _compute_W(V, C, eps=EPS):
            W = jnp.eye(C, dtype=V.dtype)

            def step(W, v):
                v = v / (jnp.linalg.norm(v) + eps)
                W = W - 2.0 * jnp.outer(v, v @ W)
                return (W, None)
            W, _ = jax.lax.scan(step, W, V)
            return W
        B, C, H, Wd = x.shape
        W = _compute_W(V, C)
        return jnp.einsum('oc,bchw->bohw', W, x)

    def _L0_ffn_ref(x, W_router, b_router, W_up, b_up, W_down, b_down):
        import jax, jax.numpy as jnp
        import numpy as np
        NUM_EXPERTS = 32
        GROUP_SIZE = 4
        NUM_GROUPS = NUM_EXPERTS // GROUP_SIZE
        C_CAP = 1.0
        B, S, H = x.shape
        bs = B * S
        E = NUM_EXPERTS
        k = min(int(bs * C_CAP) // E, bs)
        xf = x.reshape(bs, H)
        h = xf @ W_router + b_router
        Sm = jax.nn.softmax(h, axis=-1)
        G_ek, idx_ek = jax.lax.top_k(Sm.T, k)
        tokens = xf[idx_ek]
        D_FF = W_up.shape[-1]
        tok_g = tokens.reshape(NUM_GROUPS, GROUP_SIZE, k, H)
        up = jnp.einsum('gjkh,ghf->gjkf', tok_g, W_up) + b_up[:, None, None, :]
        act = jax.nn.silu(up).reshape(E, k, D_FF)
        Eout = jnp.einsum('ekf,efh->ekh', act, W_down) + b_down[:, None, :]
        weighted = G_ek[..., None] * Eout
        y = jnp.zeros((bs, H), dtype=x.dtype).at[idx_ek.reshape(-1)].add(weighted.reshape(-1, H))
        return y.reshape(B, S, H)

    def _gn(v, G=32, eps=1e-05):
        B_, C_, H_, W_ = v.shape
        g = v.reshape(B_, G, C_ // G, H_, W_)
        m = jnp.mean(g, axis=(2, 3, 4), keepdims=True)
        s = jnp.var(g, axis=(2, 3, 4), keepdims=True)
        return ((g - m) / jnp.sqrt(s + eps)).reshape(v.shape)

    def _ln_c(v, eps=1e-06):
        m = jnp.mean(v, axis=1, keepdims=True)
        s = jnp.var(v, axis=1, keepdims=True)
        return (v - m) / jnp.sqrt(s + eps)

    def _ln_t(v, eps=1e-05):
        m = jnp.mean(v, axis=-1, keepdims=True)
        s = jnp.var(v, axis=-1, keepdims=True)
        return (v - m) / jnp.sqrt(s + eps)

    def _to_tokens(v):
        B_, C_, H_, W_ = v.shape
        return v.reshape(B_, C_, H_ * W_).transpose(0, 2, 1)

    def _from_tokens(t, like):
        B_, C_, H_, W_ = like.shape
        return t.transpose(0, 2, 1).reshape(B_, C_, H_, W_)
    x = x + _L0_conv_ref(_ln_c(x), L0_conv_V)
    t = _to_tokens(x)
    t = t + _L0_ffn_ref(_ln_t(t), L0_ffn_W_router, L0_ffn_b_router, L0_ffn_W_up, L0_ffn_b_up, L0_ffn_W_down, L0_ffn_b_down)
    x = _from_tokens(t, x)
    return x

_drawn_inputs = setup_inputs


def setup_inputs(seed=0):
    import zlib

    import numpy as np

    out = dict(_drawn_inputs(seed))
    spreads = {'L0_ffn_b_router': (0.0, 0.8), 'L0_ffn_b_up': (0.0, 0.8), 'L0_ffn_b_down': (0.0, 0.765)}
    factors = {}
    for name, (base, spread) in spreads.items():
        noise = np.random.default_rng([zlib.crc32(name.encode()), seed]).standard_normal(out[name].shape)
        drawn = base * np.exp(spread * noise) if base else spread * noise
        out[name] = jnp.asarray(drawn.astype(out[name].dtype))
    for name, factor in factors.items():
        out[name] = (out[name] * factor).astype(out[name].dtype)
    return out
```

```python
import numpy as np
from contextlib import ExitStack

import concourse.bass as bass
from concourse import mybir

IMAGES, C, SIDE = 16, 128, 16
PIX = SIDE * SIDE
TOK = IMAGES * PIX
E = 32
K = TOK // E
GROUPS = 8
PER = E // GROUPS
DFF = 341
HH = 32
P = 128
CH = TOK // 512
TPC = 4
TILES = TOK // P
ROW = C + E
FF = [(0, 128), (128, 128), (256, DFF - 256)]
FR = DFF - 256
LEVELS = 5
FLOOR = 2.0 ** -102
EXP_ROUNDS = 7
MAN_ROUNDS = 23

C32 = {}
_at = 0
for _n, _w in [("ident", P), ("centre", P), ("two_eye", HH), ("merge", LEVELS * HH), ("tile_start", 1), ("slot_col", 1)]:
    C32[_n] = (_at, _at + _w)
    _at += _w
C32_COLS = _at
C16 = {}
_at = 0
for _n, _w in [("ident", P), ("tri", P), ("slots", P), ("keep", CH * P)]:
    C16[_n] = (_at, _at + _w)
    _at += _w
C16_COLS = _at
CH16 = {"same_expert": (0, P), "earlier_u": (P, 2 * P), "earlier_tile": (2 * P, 3 * P)}
CH16_COLS = 3 * P


def constants():
    i = np.arange(P)
    a = np.zeros((P, C32_COLS), np.float32)
    a[:, slice(*C32["ident"])] = np.eye(P)
    a[:, slice(*C32["centre"])] = np.eye(P) - 1.0 / P
    a[:HH, slice(*C32["two_eye"])] = 2 * np.eye(HH)
    r = np.arange(HH)
    for l in range(LEVELS):
        m = (r[:, None] >> (l + 1) == r[None, :] >> (l + 1)) & ((r[:, None] >> l & 1) == 0) & ((r[None, :] >> l & 1) == 1)
        a[:HH, C32["merge"][0] + l * HH:C32["merge"][0] + (l + 1) * HH] = m.T
    a[:, C32["tile_start"][0]] = (i % TILES) * P
    a[:, C32["slot_col"][0]] = i
    b = np.zeros((P, C16_COLS), np.float32)
    b[:, slice(*C16["ident"])] = np.eye(P)
    b[:, slice(*C16["tri"])] = i[:, None] <= i[None, :]
    b[:, slice(*C16["slots"])] = i[None, :]
    b[:, slice(*C16["keep"])] = (np.arange(CH * P) % P != 0)[None, :]
    h = np.zeros((P, CH16_COLS), np.float16)
    u, e = i // E, i % E
    h[:, 0:P] = e[:, None] == e[None, :]
    h[:, P:2 * P] = (e[:, None] == e[None, :]) & (u[:, None] < u[None, :])
    q, t = i // TILES, i % TILES
    h[:, 2 * P:] = (q[:, None] == q[None, :]) & (t[:, None] < t[None, :])
    return a, b.astype(np.float16), h


def metaformer_block(nc, x, V, w_router, b_router, w_up, b_up, w_down, b_down, c32, c16, ch16, out):
    f32, f16, i32 = mybir.dt.float32, mybir.dt.float16, mybir.dt.int32
    ALU, ACT, AX = mybir.AluOpType, mybir.ActivationFunctionType, mybir.AxisListType

    rows = nc.dram_tensor("token_rows", (TOK, ROW), f32, kind="Internal").ap()
    acc = [nc.dram_tensor(f"acc{i}", (TOK, C), f32, kind="Internal").ap() for i in range(2)]

    ctx = ExitStack()
    with ctx:
        def sb(name, shape, dt=f32):
            return ctx.enter_context(nc.sbuf_tensor(name, shape, dt))

        def pb(name, shape, dt=f32):
            return ctx.enter_context(nc.psum_tensor(name, shape, dt))

        def sem(name):
            return ctx.enter_context(nc.semaphore(name))

        k32 = sb("k32", [P, C32_COLS])
        k16 = sb("k16", [P, C16_COLS], f16)
        kh16 = sb("kh16", [P, CH16_COLS], f16)

        def c_(name, n=P):
            return k32[0:n, slice(*C32[name])]

        ident, centre = c_("ident"), c_("centre")
        ident16 = k16[:, slice(*C16["ident"])]
        tri16 = k16[:, slice(*C16["tri"])]
        slots16 = k16[:, slice(*C16["slots"])]
        keep16 = k16[:, slice(*C16["keep"])]
        same_expert = kh16[:, 0:P]
        earlier_u = kh16[:, P:2 * P]
        earlier_tile = kh16[:, 2 * P:3 * P]

        X = sb("X", [P, CH, 512])
        v_raw = sb("v_raw", [HH, C])
        v_n = sb("v_n", [HH, C])
        v_sq = sb("v_sq", [HH, C])
        v_norm = sb("v_norm", [HH, 2])
        v_t = sb("v_t", [P, HH])
        gm = sb("gm", [HH, LEVELS, HH])
        Tm = sb("Tm", [HH, HH])
        Tt = sb("Tt", [HH, HH])
        Am = sb("Am", [HH, HH])
        b1 = sb("b1", [HH, C])
        b2 = sb("b2", [HH, C])
        wT = sb("wT", [P, P])
        wM = sb("wM", [P, P])
        router = sb("router", [P, E])
        router_b = sb("router_b", [P, E])
        wb = sb("wb", [P, E])
        stage_w = sb("stage_w", [P, C + 2 * E])
        bn1 = sb("bn1", [P, 2, TPC, 6])
        mv1 = sb("mv1", [P, 2, TPC, 2])
        rs1 = sb("rs1", [P, CH, TPC])
        ve1 = sb("ve1", [P, 2, TPC])
        bn2 = sb("bn2", [P, 2, TPC, 6])
        mv2 = sb("mv2", [P, 2, TPC, 2])
        rs2 = sb("rs2", [P, CH, TPC])
        nb2 = sb("nb2", [P, CH, TPC])
        ve2 = sb("ve2", [P, 2, TPC])
        mhalf = sb("mhalf", [P, TPC])
        xT = sb("xT", [P, 2, TPC, C])
        x1 = sb("x1", [P, TILES, C])
        xf = sb("xf", [P, TILES, C])
        lg = sb("lg", [P, 2, TPC, E])
        mx = sb("mx", [P, 2, TPC])
        pr = sb("pr", [P, 2, TPC, E])
        sm = sb("sm", [P, 2, TPC])
        rsm = sb("rsm", [P, 2, TPC])
        S = sb("S", [P, TILES, E])
        key = sb("key", [P, CH, P])
        junk = sb("junk", [P, CH * P], f16)
        cand = sb("cand", [P, 1])
        step = sb("step", [P, 1])
        hit = sb("hit", [P, 1])
        cnt = sb("cnt", [P, 1], f16)
        gt = sb("gt", [P, CH * P], f16)
        eq = sb("eq", [P, CH * P], f16)
        rank = sb("rank", [P, CH, P], f16)
        tie_tot = sb("tie_tot", [P, CH], f16)
        tie_inc = sb("tie_inc", [P, CH], f16)
        tie_exc = sb("tie_exc", [P, CH], f16)
        one8 = sb("one8", [P, CH])
        lim = sb("lim", [P, CH])
        tie_ok = sb("tie_ok", [P, CH, P], f16)
        sel = sb("sel", [P, CH * P], f16)
        selT = sb("selT", [P, E, TILES], f16)
        tot = sb("tot", [P, GROUPS], f16)
        base = sb("base", [P, GROUPS])
        bend = sb("bend", [P, GROUPS])
        cum = sb("cum", [P, GROUPS, P + 2], f16)
        after = sb("after", [P, GROUPS, P], f16)
        onehot = sb("onehot", [P, GROUPS, P], f16)
        junk2 = sb("junk2", [P, P], f16)
        below = sb("below", [P, E])
        idx = sb("idx", [P, E], i32)
        wup = sb("wup", [P, GROUPS, DFF])
        bup = sb("bup", [P, 3, GROUPS])
        wdn = sb("wdn", [P, E, 2, C])
        wdn2 = sb("wdn2", [FR + 1, E, C])
        xg = sb("xg", [P, E, ROW])
        xgT = sb("xgT", [P, 2, 512])
        act = sb("act", [P, 2, 3, 512])
        eo = X[:, :, :].rearrange("p g (q c) -> p (g q) c", c=C)
        zero = sb("zero", [P, 1024])
        y0, y1, ysum, yo = x1, xf, x1, X

        PZ = pb("PZ", [P, 4, 512])
        PT = pb("PT", [P, 2, 512])
        PM = pb("PM", [P, 2, 512])

        s_const = sem("constants_loaded")
        s_v = sem("v_loaded")
        s_router = sem("router_loaded")
        s_x = [sem(f"x_loaded{g}") for g in range(CH)]
        s_wup = sem("w_up_loaded")
        s_wdn = sem("w_down_loaded")
        s_bup = sem("b_up_loaded")
        s_zero = sem("zero_ready")
        s_set = sem("w_setup_pe")
        s_setv = sem("w_setup_dve")
        s_seta = sem("w_setup_act")
        s_fill = sem("fills_ready")
        s_wst = sem("stage_w_ready")
        dch = sem("dve_chain")
        ach = sem("act_chain")
        pch = sem("pool_chain")
        s_xt = sem("x_transposed")
        s_xts = sem("x_transposed_in_sbuf")
        s_z = sem("mixed_ready")
        s_st1 = sem("channel_stats_ready")
        s_rs1 = sem("channel_rstd_ready")
        s_x1 = sem("residual_ready")
        s_st2 = sem("token_stats_ready")
        s_rs2 = sem("token_rstd_ready")
        s_xf = sem("normalised_ready")
        s_zfree = sem("mixed_used")
        s_lg = sem("logits_ready")
        s_exp = sem("exp_ready")
        s_S = sem("softmax_ready")
        s_sT = sem("softmax_transposed")
        s_key = sem("keys_ready")
        s_rows_x = sem("rows_x_stored")
        s_rows_s = sem("rows_s_stored")
        s_acc0 = sem("acc0_filled")
        s_acc1 = sem("acc1_filled")
        s_cnt = sem("counts_ready")
        s_sum = sem("count_sums_ready")
        s_tie = sem("tie_totals_ready")
        s_tieb = sem("tie_bases_ready")
        s_sel = sem("selection_ready")
        s_selp = sem("selection_transposed")
        s_selT = sem("selection_transposed_in_sbuf")
        s_cum = sem("prefix_counts_ready")
        s_tot = sem("tile_totals_ready")
        s_base = sem("tile_bases_ready")
        s_oh = sem("onehot_ready")
        s_find = sem("slot_rows_ready")
        s_idx = sem("indices_ready")
        s_g = [sem(f"gathered{g}") for g in range(GROUPS)]
        s_gT = sem("gathered_transposed")
        s_gTs = sem("gathered_transposed_in_sbuf")
        s_up = sem("up_ready")
        s_act = sem("activated")
        s_dn = sem("down_ready")
        s_eo = sem("expert_out_ready")
        s_sc = [sem(f"scattered{i}") for i in range(2)]
        s_y = [sem(f"y_loaded{g}") for g in range(CH)]
        s_ys = sem("y_summed")
        s_yT = sem("y_transposed")
        s_yo = sem("y_out_ready")
        s_out = sem("out_stored")

        block = ctx.enter_context(nc.Block())

        x_v = x.rearrange("(g b) c n -> g c b n", b=2)
        out_v = out.rearrange("(g b) c n -> g c b n", b=2)
        rows_v = rows.rearrange("(g u p) c -> g p u c", u=TPC, p=P)
        acc_v = [a.rearrange("(g u p) c -> g p u c", u=TPC, p=P) for a in acc]

        def per_chunk(t, g):
            return t[:, g * TPC:(g + 1) * TPC, :]

        @block.sync
        def _(sp):
            sp.dma_start(v_raw[:, :], V).then_inc(s_v, 16)
            sp.dma_start(k32[:, :], c32).then_inc(s_const, 16)
            for g in range(CH):
                sp.dma_start(X[:, g, :].rearrange("p (b n) -> p b n", b=2), x_v[g]).then_inc(s_x[g], 16)
                if g == 0:
                    sp.dma_start(k16[:, :], c16).then_inc(s_const, 16)
                    sp.dma_start(kh16[:, :], ch16).then_inc(s_const, 16)
            sp.dma_start(wup[:, :, :], w_up.rearrange("g c f -> c g f")).then_inc(s_wup, 16)
            for j, (f0, fn) in enumerate(FF):
                sp.dma_start(bup[0:fn, j, :], b_up[f0:f0 + fn, :]).then_inc(s_bup, 16)
            for j in range(2):
                sp.dma_start(wdn[:, :, j, :], w_down[:, j * P:(j + 1) * P, :].rearrange("e f c -> f e c")).then_inc(s_wdn, 16)
            sp.dma_start(wdn2[0:FR, :, :], w_down[:, 2 * P:DFF, :].rearrange("e f c -> f e c")).then_inc(s_wdn, 16)
            sp.dma_start(wdn2[FR:FR + 1, :, :], b_down.rearrange("(o e) c -> o e c", o=1)).then_inc(s_wdn, 16)
            sp.wait_ge(s_zero, 1)
            for q in range(4):
                sp.dma_start(acc[1][q * 1024:(q + 1) * 1024, :].rearrange("(p k) c -> p (k c)", p=P), zero[:, :]).then_inc(s_acc1, 16)
            for g in range(CH):
                sp.wait_ge(s_xf, TPC * (g + 1))
                sp.dma_start(rows_v[g, :, :, 0:C], per_chunk(xf, g)).then_inc(s_rows_x, 16)
            for i in range(2):
                sp.wait_ge(s_sc[i], 16 * (E // 2))
            for g in range(CH):
                sp.dma_start(per_chunk(y0, g), acc_v[0][g]).then_inc(s_y[g], 16)
                if g == 0:
                    sp.wait_ge(s_rows_x, 16 * CH)
                sp.dma_start(per_chunk(y1, g), acc_v[1][g]).then_inc(s_y[g], 16)
            for g in range(CH):
                sp.wait_ge(s_yo, g + 1)
                sp.dma_start(out_v[g], yo[:, g, :].rearrange("p (b n) -> p b n", b=2)).then_inc(s_out, 16)
            sp.wait_ge(s_out, 16 * CH)

        @block.gpsimd
        def _(pool):
            nch = [0]

            def link(ins):
                nch[0] += 1
                ins.then_inc(pch, 1)
                pool.wait_ge(pch, nch[0])

            nc.gpsimd.memset(zero[:, :], 0.0).then_inc(s_zero, 1)
            nc.gpsimd.memset(one8[:, :], 1.0).then_inc(s_fill, 1)
            nc.gpsimd.memset(act[:, :, :, :], 1.0).then_inc(s_fill, 1)
            link(nc.gpsimd.memset(mhalf[:, :], -0.5))
            for g in range(CH + 1):
                if g < CH:
                    pool.wait_ge(s_st1, g + 1)
                    link(nc.gpsimd.tensor_scalar(ve1[:, g % 2, :], mv1[:, g % 2, :, 1], 1e-6, None, ALU.add))
                    nc.gpsimd.tensor_tensor(rs1[:, g, :], ve1[:, g % 2, :], mhalf[:, :], ALU.pow).then_inc(s_rs1, 1)
                if g >= 1:
                    h = g - 1
                    pool.wait_ge(s_st2, h + 1)
                    link(nc.gpsimd.tensor_scalar(ve2[:, h % 2, :], mv2[:, h % 2, :, 1], 1e-5, None, ALU.add))
                    link(nc.gpsimd.tensor_tensor(rs2[:, h, :], ve2[:, h % 2, :], mhalf[:, :], ALU.pow))
                    link(nc.gpsimd.tensor_tensor(nb2[:, h, :], mv2[:, h % 2, :, 0], rs2[:, h, :], ALU.mult))
                    nc.gpsimd.tensor_scalar(nb2[:, h, :], nb2[:, h, :], -1.0, None, ALU.mult).then_inc(s_rs2, 1)
            for g in range(CH):
                pool.wait_ge(s_x1, TPC * (g + 1))
                pool.dma_start(acc_v[0][g], per_chunk(x1, g)).then_inc(s_acc0, 16)
            for g in range(CH):
                pool.wait_ge(s_S, g + 1)
                pool.dma_start(rows_v[g, :, :, C:ROW], per_chunk(S, g)).then_inc(s_rows_s, 16)

            def gather(g):
                for e in range(g * PER, (g + 1) * PER):
                    pool.wait_ge(s_idx, e + 1)
                    nc.gpsimd.indirect_dma_start(
                        out=xg[:, e, :], out_offset=None, in_=rows[:, :],
                        in_offset=bass.IndirectOffsetOnAxis(ap=idx[:, e:e + 1], axis=0)).then_inc(s_g[g], 16)

            def scatter(g):
                for e in range(g * PER, (g + 1) * PER):
                    pool.wait_ge(s_eo, e + 1)
                    if e >= 2:
                        pool.wait_ge(s_sc[e % 2], 16 * (e // 2))
                    nc.gpsimd.indirect_dma_start(
                        out=acc[e % 2][:, :], out_offset=bass.IndirectOffsetOnAxis(ap=idx[:, e:e + 1], axis=0),
                        in_=eo[:, e, :], in_offset=None, compute_op=ALU.add).then_inc(s_sc[e % 2], 16)

            pool.wait_ge(s_rows_x, 16 * CH)
            pool.wait_ge(s_rows_s, 16 * CH)
            gather(0)
            gather(1)
            pool.wait_ge(s_acc0, 16 * CH)
            pool.wait_ge(s_acc1, 16 * 4)
            for g in range(GROUPS):
                if g + 2 < GROUPS:
                    gather(g + 2)
                scatter(g)

        @block.scalar
        def _(a):
            nch = [0]

            def link(ins):
                nch[0] += 1
                ins.then_inc(ach, 1)
                a.wait_ge(ach, nch[0])

            a.dma_start(router[:, :], w_router).then_inc(s_router, 16)
            a.dma_start(router_b[:, :], b_router.rearrange("(o e) -> o e", o=1).to_broadcast([P, E])).then_inc(s_router, 16)
            a.wait_ge(s_v, 16)
            link(nc.scalar.activation(v_sq[:, :], v_raw[:, :], ACT.Square, accum_out=v_norm[:, 0:1]))
            nc.scalar.activation(v_norm[:, 1:2], v_norm[:, 0:1], ACT.Sqrt).then_inc(s_seta, 1)

            def normalise(g):
                a.wait_ge(s_rs2, g + 1)
                for u in range(TPC):
                    nc.scalar.activation(xf[:, g * TPC + u, :], x1[:, g * TPC + u, :], ACT.Identity,
                                         bias=nb2[:, g, u:u + 1], scale=rs2[:, g, u:u + 1]).then_inc(s_xf, 1)

            def exps(g):
                a.wait_ge(s_lg, g + 1)
                if g >= 2:
                    a.wait_ge(s_S, g - 1)
                nc.scalar.activation(pr[:, g % 2, :, :], lg[:, g % 2, :, :], ACT.Exp).then_inc(s_exp, 1)

            def copy_x(g):
                a.wait_ge(s_xt, g + 1)
                if g >= 2:
                    a.wait_ge(s_x1, TPC * (g - 1))
                nc.scalar.activation(xT[:, g % 2, :, :], PT[:, g % 2, :].rearrange("p (u c) -> p u c", u=TPC), ACT.Copy).then_inc(s_xts, 1)

            for g in range(CH + 2):
                if g < CH:
                    copy_x(g)
                if 1 <= g <= CH:
                    normalise(g - 1)
                if g >= 2:
                    exps(g - 2)
            for g in range(GROUPS):
                a.wait_ge(s_gT, g + 1)
                if g >= 2:
                    a.wait_ge(s_up, 3 * (g - 1))
                nc.scalar.activation(xgT[:, g % 2, :], PT[:, 0, :], ACT.Copy).then_inc(s_gTs, 1)
                if g == 0:
                    a.wait_ge(s_bup, 48)
                    a.wait_ge(s_fill, 2)
                for j, (f0, fn) in enumerate(FF):
                    a.wait_ge(s_up, 3 * g + j + 1)
                    if g >= 2 and j == 0:
                        a.wait_ge(s_dn, PER * (g - 1))
                    src = PT[0:fn, 1, :] if (3 * g + j) % 2 == 0 else PM[0:fn, 0, :]
                    nc.scalar.activation(act[0:fn, g % 2, j, :], src, ACT.Silu, bias=bup[0:fn, j, g:g + 1]).then_inc(s_act, 1)
            for g in range(CH):
                a.wait_ge(s_yT, g + 1)
                nc.scalar.activation(yo[:, g, :], PT[:, g % 2, :], ACT.Copy).then_inc(s_yo, 1)

        @block.vector
        def _(v):
            nch = [0]

            def link(ins):
                nch[0] += 1
                ins.then_inc(dch, 1)
                v.wait_ge(dch, nch[0])

            v.wait_ge(s_seta, 1)
            link(nc.vector.tensor_scalar(v_norm[:, 1:2], v_norm[:, 1:2], 1e-8, None, ALU.add))
            link(nc.vector.reciprocal(v_norm[:, 0:1], v_norm[:, 1:2]))
            nc.vector.tensor_scalar(v_n[:, :], v_raw[:, :], v_norm[:, 0:1], None, ALU.mult).then_inc(s_setv, 1)
            v.wait_ge(s_set, 1)
            nc.vector.tensor_copy(v_t[:, :], PM[:, 0, 0:HH]).then_inc(s_setv, 1)
            v.wait_ge(s_const, 48)
            nc.vector.tensor_copy(Tm[:, :], c_("two_eye", HH))
            nc.vector.tensor_copy(Tt[:, :], c_("two_eye", HH))
            v.wait_ge(s_set, 2)
            nc.vector.tensor_tensor(gm[:, :, :], PM[0:HH, 1, 0:HH].unsqueeze(1).to_broadcast([HH, LEVELS, HH]),
                                    c_("merge", HH).rearrange("p (l h) -> p l h", l=LEVELS), ALU.mult).then_inc(s_setv, 1)
            for l in range(LEVELS):
                v.wait_ge(s_set, 3 + 2 * l)
                nc.vector.tensor_copy(Am[:, :], PM[0:HH, 0, 0:HH]).then_inc(s_setv, 1)
                v.wait_ge(s_set, 4 + 2 * l)
                nc.vector.tensor_tensor(Tm[:, :], Tm[:, :], PM[0:HH, 1, 0:HH], ALU.subtract)
                nc.vector.tensor_tensor(Tt[:, :], Tt[:, :], PM[0:HH, 1, HH:2 * HH], ALU.subtract).then_inc(s_setv, 1)
            n = 2 + 2 * LEVELS
            v.wait_ge(s_set, n + 1)
            nc.vector.tensor_copy(b1[:, :], PM[0:HH, 0, 0:C])
            nc.vector.tensor_copy(b2[:, :], PM[0:HH, 0, C:2 * C]).then_inc(s_setv, 1)
            v.wait_ge(s_set, n + 2)
            nc.vector.tensor_tensor(wT[:, :], ident, PM[:, 1, 0:C], ALU.subtract)
            nc.vector.tensor_tensor(wM[:, :], ident, PM[:, 1, C:2 * C], ALU.subtract)
            nc.vector.tensor_copy(stage_w[:, C + E:C + 2 * E], PM[:, 1, 2 * C:2 * C + E]).then_inc(s_setv, 1)
            v.wait_ge(s_set, n + 3)
            nc.vector.tensor_copy(stage_w[:, 0:C], PM[:, 0, 0:C])
            nc.vector.tensor_copy(wb[:, :], PM[:, 0, C:C + E]).then_inc(s_setv, 1)
            v.wait_ge(s_set, n + 4)
            nc.vector.tensor_copy(stage_w[:, C:C + E], PM[:, 1, 0:E]).then_inc(s_wst, 1)

            def stats1(g):
                v.wait_ge(s_xts, g + 1)
                for u in range(TPC):
                    ins = nc.vector.bn_stats(bn1[:, g % 2, u, :], xT[:, g % 2, u, :])
                link(ins)
                if g >= 2:
                    v.wait_ge(s_rs1, g - 1)
                for u in range(TPC):
                    ins = nc.vector.bn_aggr(mv1[:, g % 2, u, :], bn1[:, g % 2, u, :])
                ins.then_inc(s_st1, 1)

            def zview(g, lo, n):
                return PZ[:, 2 * (g % 2):2 * (g % 2) + 2, 0:2 * (C + 2 * E)].rearrange("p k (w c) -> p k w c", w=2)[:, :, :, lo:lo + n]

            def residual(g):
                v.wait_ge(s_z, g + 1)
                v.wait_ge(s_rs1, g + 1)
                for u in range(TPC):
                    z = PZ[:, 2 * (g % 2) + u // 2, (u % 2) * (C + 2 * E):(u % 2) * (C + 2 * E) + C]
                    nc.vector.scalar_tensor_tensor(x1[:, g * TPC + u, :], z, rs1[:, g, u:u + 1], xT[:, g % 2, u, :],
                                                   ALU.mult, ALU.add).then_inc(s_x1, 1)
                v.wait_ge(s_x1, TPC * (g + 1))
                for u in range(TPC):
                    ins = nc.vector.bn_stats(bn2[:, g % 2, u, :], x1[:, g * TPC + u, :])
                link(ins)
                if g >= 2:
                    v.wait_ge(s_rs2, g - 1)
                for u in range(TPC):
                    ins = nc.vector.bn_aggr(mv2[:, g % 2, u, :], bn2[:, g % 2, u, :])
                ins.then_inc(s_st2, 1)

            def b4(t):
                return t.unsqueeze(2).to_broadcast([P, TPC, E])

            def b22(t):
                return t.rearrange("p (k w) -> p k w", k=2).unsqueeze(3).to_broadcast([P, 2, 2, E])

            def logits(g):
                L = lg[:, g % 2, :, :]
                L22 = L.rearrange("p (k w) e -> p k w e", k=2)
                link(nc.vector.tensor_tensor(L22, zview(g, C, E), b22(rs1[:, g, :]), ALU.mult))
                ins = nc.vector.tensor_tensor(L22, L22, zview(g, C + E, E), ALU.add)
                ins.then_inc(s_zfree, 1)
                v.wait_ge(s_zfree, g + 1)
                v.wait_ge(s_rs2, g + 1)
                link(nc.vector.tensor_tensor(L, L, b4(rs2[:, g, :]), ALU.mult))
                link(nc.vector.tensor_tensor(L, L, router_b[:, :].unsqueeze(1).to_broadcast([P, TPC, E]), ALU.add))
                link(nc.vector.tensor_reduce(mx[:, g % 2, :], L, AX.X, ALU.max))
                nc.vector.tensor_tensor(L, L, b4(mx[:, g % 2, :]), ALU.subtract).then_inc(s_lg, 1)

            def softmax(g):
                v.wait_ge(s_exp, g + 1)
                link(nc.vector.tensor_reduce(sm[:, g % 2, :], pr[:, g % 2, :, :], AX.X, ALU.add))
                link(nc.vector.reciprocal(rsm[:, g % 2, :], sm[:, g % 2, :]))
                nc.vector.tensor_tensor(per_chunk(S, g), pr[:, g % 2, :, :], b4(rsm[:, g % 2, :]), ALU.mult).then_inc(s_S, 1)

            def keys(g):
                v.wait_ge(s_sT, g + 1)
                nc.vector.tensor_scalar(key[:, g, :], PM[:, g % 2, 0:P], FLOOR, None, ALU.max).then_inc(s_key, 1)

            v.wait_ge(s_router, 32)
            for g in range(CH + 3):
                if g < CH:
                    stats1(g)
                if 1 <= g <= CH:
                    residual(g - 1)
                    logits(g - 1)
                if 2 <= g <= CH + 1:
                    softmax(g - 2)
                if g >= 3:
                    keys(g - 3)

            v.wait_ge(s_key, CH)
            link(nc.vector.memset(cand[:, :], FLOOR * 2.0 ** 64))
            keyf = key[:, :, :].rearrange("p g n -> p (g n)")

            def count():
                nc.vector.tensor_scalar(junk[:, :], keyf, cand[:, 0:1], None, ALU.is_ge, ALU.add, accum_out=cnt[:, 0:1]).then_inc(s_cnt, 1)

            for j in range(EXP_ROUNDS):
                count()
                v.wait_ge(s_sum, j + 1)
                f = 2.0 ** (2 ** (EXP_ROUNDS - 2 - j)) if j < EXP_ROUNDS - 1 else 1.0
                inv = 1.0 / f if j < EXP_ROUNDS - 1 else 0.5
                link(nc.vector.tensor_scalar(hit[:, :], PM[:, 0, 0:1], float(K), float(np.float32(f - inv)), ALU.is_ge, ALU.mult))
                link(nc.vector.scalar_tensor_tensor(cand[:, :], hit[:, :], inv, cand[:, :], ALU.add, ALU.mult))
            link(nc.vector.tensor_scalar(step[:, :], cand[:, :], 0.5, None, ALU.mult))
            link(nc.vector.tensor_scalar(cand[:, :], cand[:, :], 1.5, None, ALU.mult))
            base_n = nch[0]
            with v.Fori(0, MAN_ROUNDS - 1) as i:
                count()
                v.wait_ge(s_sum, i + EXP_ROUNDS + 1)
                nc.vector.tensor_scalar(hit[:, :], PM[:, 0, 0:1], float(K), 0.5, ALU.is_ge, ALU.subtract).then_inc(dch, 1)
                v.wait_ge(dch, i * 2 + base_n + 1)
                nc.vector.scalar_tensor_tensor(cand[:, :], hit[:, :], step[:, 0:1], cand[:, :], ALU.mult, ALU.add)
                nc.vector.tensor_scalar(step[:, :], step[:, :], 0.5, None, ALU.mult).then_inc(dch, 1)
                v.wait_ge(dch, i * 2 + base_n + 2)
            nch[0] = base_n + 2 * (MAN_ROUNDS - 1)
            count()
            v.wait_ge(s_sum, EXP_ROUNDS + MAN_ROUNDS)
            link(nc.vector.tensor_scalar(hit[:, :], PM[:, 0, 0:1], float(K), -1.0, ALU.is_ge, ALU.add))
            link(nc.vector.scalar_tensor_tensor(cand[:, :], hit[:, :], step[:, 0:1], cand[:, :], ALU.mult, ALU.add))

            nc.vector.tensor_scalar(gt[:, :], keyf, cand[:, 0:1], None, ALU.is_gt, ALU.add, accum_out=cnt[:, 0:1]).then_inc(s_cnt, 1)
            link(nc.vector.tensor_scalar(eq[:, :], keyf, cand[:, 0:1], None, ALU.is_equal))
            link(nc.vector.tensor_tensor_scan(rank[:, :, :].rearrange("p g n -> p (g n)"), keep16, eq[:, :], 0.0, ALU.mult, ALU.add))
            link(nc.vector.tensor_copy(tie_tot[:, :], rank[:, :, P - 1]))
            v.wait_ge(s_fill, 2)
            link(nc.vector.tensor_tensor_scan(tie_inc[:, :], one8[:, :], tie_tot[:, :], 0.0, ALU.mult, ALU.add))
            nc.vector.tensor_tensor(tie_exc[:, :], tie_inc[:, :], tie_tot[:, :], ALU.subtract).then_inc(s_tie, 1)
            v.wait_ge(s_tieb, 1)
            link(nc.vector.tensor_scalar(lim[:, :], PM[:, 1, 0:CH], -1.0, float(K), ALU.mult, ALU.add))
            link(nc.vector.tensor_scalar(lim[:, :], lim[:, :], PM[:, 0, 0:1], None, ALU.subtract))
            link(nc.vector.tensor_tensor(tie_ok[:, :, :], rank[:, :, :], lim[:, :].unsqueeze(2).to_broadcast([P, CH, P]), ALU.is_le))
            link(nc.vector.tensor_tensor(eq[:, :], eq[:, :], tie_ok[:, :, :].rearrange("p g n -> p (g n)"), ALU.mult))
            nc.vector.tensor_tensor(sel[:, :], gt[:, :], eq[:, :], ALU.add).then_inc(s_sel, 1)
            v.wait_ge(s_selp, 1)
            nc.vector.tensor_copy(selT[:, :, :].rearrange("p e (g u) -> p g u e", u=TPC),
                                  PT[:, 0, :].bitcast(f16).rearrange("p (g u e) -> p g u e", g=CH, u=TPC)).then_inc(s_selT, 1)

            v.wait_ge(s_cum, 1)
            link(nc.vector.tensor_copy(tot[:, :], PZ[:, 0:2, :].rearrange("p k (g n) -> p (k g) n", n=P)[:, :, P - 1]))
            nc.vector.tensor_copy(cum[:, :, P:P + 1], c_("tile_start").unsqueeze(1).to_broadcast([P, GROUPS, 1])).then_inc(s_tot, 1)
            v.wait_ge(s_base, 1)
            link(nc.vector.tensor_copy(base[:, :], PM[:, 1, 0:GROUPS]))
            nc.vector.tensor_tensor(bend[:, :], base[:, :], tot[:, :], ALU.add)
            link(nc.vector.tensor_tensor(cum[:, :, 0:P], PZ[:, 0:2, :].rearrange("p k (g n) -> p (k g) n", n=P),
                                         base[:, :].unsqueeze(2).to_broadcast([P, GROUPS, P]), ALU.add))
            for g in range(GROUPS):
                link(nc.vector.tensor_scalar(after[:, g, :], slots16, base[:, g:g + 1], None, ALU.is_ge))
                nc.vector.scalar_tensor_tensor(onehot[:, g, :], slots16, bend[:, g:g + 1], after[:, g, :], ALU.is_lt, ALU.mult).then_inc(s_oh, 1)
            for e in range(E):
                v.wait_ge(s_find, e + 1)
                link(nc.vector.tensor_scalar(junk2[:, :], PZ[:, e % PER, 0:P], c_("slot_col"), None, ALU.is_le, ALU.add,
                                             accum_out=below[:, e:e + 1]))
                nc.vector.tensor_tensor(idx[:, e:e + 1], below[:, e:e + 1], PZ[:, e % PER, P:P + 1], ALU.add).then_inc(s_idx, 1)

            for e in range(E):
                v.wait_ge(s_dn, e + 1)
                nc.vector.tensor_scalar(eo[:, e, :], PZ[:, e % PER, 0:C], xg[:, e, C + e:C + e + 1], None, ALU.mult).then_inc(s_eo, 1)
            for g in range(CH):
                v.wait_ge(s_y[g], 32)
                nc.vector.tensor_tensor(per_chunk(ysum, g), per_chunk(y0, g), per_chunk(y1, g), ALU.add).then_inc(s_ys, 1)

        @block.tensor
        def _(pe):
            mm = nc.tensor.matmul
            pe.wait_ge(s_const, 48)
            pe.wait_ge(s_setv, 1)
            nc.tensor.transpose(PM[:, 0, 0:HH], v_n[:, :], c_("ident", HH)[:, 0:HH]).then_inc(s_set, 1)
            pe.wait_ge(s_setv, 2)
            mm(PM[0:HH, 1, 0:HH], v_t[:, :], v_t[:, :], start=True, stop=True).then_inc(s_set, 1)
            pe.wait_ge(s_setv, 3)
            for l in range(LEVELS):
                mm(PM[0:HH, 0, 0:HH], gm[:, l, :], Tm[:, :], start=True, stop=True).then_inc(s_set, 1)
                pe.wait_ge(s_setv, 4 + 2 * l)
                mm(PM[0:HH, 1, 0:HH], Tt[:, :], Am[:, :], start=True, stop=True)
                mm(PM[0:HH, 1, HH:2 * HH], Am[:, :], Tt[:, :], start=True, stop=True).then_inc(s_set, 1)
                pe.wait_ge(s_setv, 5 + 2 * l)
            n = 3 + 2 * LEVELS
            mm(PM[0:HH, 0, 0:C], Tt[:, :], v_n[:, :], start=True, stop=True)
            mm(PM[0:HH, 0, C:2 * C], Tm[:, :], v_n[:, :], start=True, stop=True).then_inc(s_set, 1)
            pe.wait_ge(s_setv, n + 1)
            pe.wait_ge(s_router, 32)
            mm(PM[:, 1, 0:C], v_n[:, :], b1[:, :], start=True, stop=True)
            mm(PM[:, 1, C:2 * C], v_n[:, :], b2[:, :], start=True, stop=True)
            mm(PM[:, 1, 2 * C:2 * C + E], centre, router[:, :], start=True, stop=True).then_inc(s_set, 1)
            pe.wait_ge(s_setv, n + 2)
            mm(PM[:, 0, 0:C], centre, wT[:, :], start=True, stop=True)
            mm(PM[:, 0, C:C + E], wM[:, :], stage_w[:, C + E:C + 2 * E], start=True, stop=True).then_inc(s_set, 1)
            pe.wait_ge(s_setv, n + 3)
            mm(PM[:, 1, 0:E], centre, wb[:, :], start=True, stop=True).then_inc(s_set, 1)

            def keys_transpose(g):
                pe.wait_ge(s_S, g + 1)
                if g >= 2:
                    pe.wait_ge(s_key, g - 1)
                nc.tensor.transpose(PM[:, g % 2, 0:P], per_chunk(S, g).rearrange("p u e -> p (u e)"), ident).then_inc(s_sT, 1)

            def x_transpose(g):
                pe.wait_ge(s_x[g], 16)
                if g >= 2:
                    pe.wait_ge(s_xts, g - 1)
                for u in range(TPC):
                    ins = nc.tensor.transpose(PT[:, g % 2, u * P:(u + 1) * P], X[:, g, u * P:(u + 1) * P], ident)
                ins.then_inc(s_xt, 1)

            x_transpose(0)
            x_transpose(1)
            pe.wait_ge(s_wst, 1)
            for g in range(CH + 2):
                if g < CH:
                    if g >= 2:
                        x_transpose(g)
                        pe.wait_ge(s_zfree, g - 1)
                    W_ = C + 2 * E
                    for u in range(TPC):
                        ins = mm(PZ[:, 2 * (g % 2) + u // 2, (u % 2) * W_:(u % 2 + 1) * W_], X[:, g, u * P:(u + 1) * P], stage_w[:, :],
                                 start=True, stop=True)
                    ins.then_inc(s_z, 1)
                if g >= 2:
                    keys_transpose(g - 2)

            pe.wait_ge(s_key, CH)
            with pe.Fori(0, EXP_ROUNDS + MAN_ROUNDS) as i:
                pe.wait_ge(s_cnt, i + 1)
                mm(PM[:, 0, 0:1], same_expert, cnt[:, 0:1], start=True, stop=True).then_inc(s_sum, 1)
            pe.wait_ge(s_cnt, EXP_ROUNDS + MAN_ROUNDS + 1)
            mm(PM[:, 0, 0:1], same_expert, cnt[:, 0:1], start=True, stop=True)
            pe.wait_ge(s_tie, 1)
            mm(PM[:, 1, 0:CH], same_expert, tie_exc[:, :], start=True, stop=False)
            mm(PM[:, 1, 0:CH], earlier_u, tie_tot[:, :], start=False, stop=True).then_inc(s_tieb, 1)
            pe.wait_ge(s_sel, 1)
            for g in range(CH):
                ins = nc.tensor.transpose(PT[:, 0, :].bitcast(f16)[:, g * P:(g + 1) * P], sel[:, g * P:(g + 1) * P], ident16)
            ins.then_inc(s_selp, 1)
            pe.wait_ge(s_selT, 1)
            for g in range(GROUPS):
                ins = mm(PZ[:, g // 4, (g % 4) * P:(g % 4 + 1) * P], selT[:, g * PER:(g + 1) * PER, :].rearrange("p e t -> p (e t)"), tri16,
                         start=True, stop=True)
            ins.then_inc(s_cum, 1)
            pe.wait_ge(s_tot, 1)
            mm(PM[:, 1, 0:GROUPS], earlier_tile, tot[:, :], start=True, stop=True).then_inc(s_base, 1)
            for g in range(GROUPS):
                pe.wait_ge(s_oh, g + 1)
                for q in range(PER):
                    if g >= 1:
                        pe.wait_ge(s_idx, (g - 1) * PER + q + 1)
                    r = slice(q * TILES, (q + 1) * TILES)
                    mm(PZ[:, q, 0:P + 1], onehot[r, g, :], cum[r, g, 0:P + 1], start=True, stop=True).then_inc(s_find, 1)

            def gathered_transpose(g):
                pe.wait_ge(s_g[g], 16 * PER)
                if g >= 1:
                    pe.wait_ge(s_gTs, g)
                for q in range(PER):
                    ins = nc.tensor.transpose(PT[:, 0, q * P:(q + 1) * P], xg[:, g * PER + q, 0:C], ident)
                ins.then_inc(s_gT, 1)

            def up(g):
                pe.wait_ge(s_gTs, g + 1)
                for j, (f0, fn) in enumerate(FF):
                    n = 3 * g + j
                    if n >= 2:
                        pe.wait_ge(s_act, n - 1)
                    dst = PT[0:fn, 1, :] if n % 2 == 0 else PM[0:fn, 0, :]
                    mm(dst, wup[:, g, f0:f0 + fn], xgT[:, g % 2, :], start=True, stop=True).then_inc(s_up, 1)

            def down(g):
                pe.wait_ge(s_act, 3 * (g + 1))
                for q in range(PER):
                    e = g * PER + q
                    if g >= 1:
                        pe.wait_ge(s_eo, e - PER + 1)
                    for j in range(3):
                        w = wdn[:, e, j, :] if j < 2 else wdn2[:, e, :]
                        k = P if j < 2 else FR + 1
                        ins = mm(PZ[:, q, 0:C], act[0:k, g % 2, j, q * P:(q + 1) * P], w, start=(j == 0), stop=(j == 2))
                    ins.then_inc(s_dn, 1)

            pe.wait_ge(s_idx, E)
            pe.wait_ge(s_wup, 16)
            pe.wait_ge(s_wdn, 64)
            for g in range(GROUPS + 1):
                if g < GROUPS:
                    gathered_transpose(g)
                    up(g)
                if g >= 1:
                    down(g - 1)
            for g in range(CH):
                pe.wait_ge(s_ys, g + 1)
                if g >= 2:
                    pe.wait_ge(s_yo, g - 1)
                for u in range(TPC):
                    ins = nc.tensor.transpose(PT[:, g % 2, u * P:(u + 1) * P], ysum[:, g * TPC + u, :], ident)
                ins.then_inc(s_yT, 1)


_INS = ["x", "L0_conv_V", "L0_ffn_W_router", "L0_ffn_b_router", "L0_ffn_W_up", "L0_ffn_b_up", "L0_ffn_W_down", "L0_ffn_b_down"]


def kernel(**inputs):
    import concourse.bacc as bacc
    from concourse.bass_utils import run_bass_kernel_spmd as run

    nc = bacc.Bacc("TRN2", target_bir_lowering=False, num_devices=1)
    arrays = {name: np.ascontiguousarray(inputs[name]) for name in _INS}
    arrays["x"] = arrays["x"].reshape(IMAGES, C, PIX)
    arrays["L0_ffn_b_up"] = np.ascontiguousarray(arrays["L0_ffn_b_up"].T)
    arrays.update(zip(("const_f32", "const_f16", "const_counting"), constants()))
    args = [nc.dram_tensor(f"in_{n}", a.shape, mybir.dt.from_np(a.dtype), kind="ExternalInput").ap() for n, a in arrays.items()]
    out = nc.dram_tensor("out_0", (IMAGES, C, PIX), mybir.dt.float32, kind="ExternalOutput").ap()
    metaformer_block(nc, *args, out)
    r = run(nc, [{f"in_{n}": a for n, a in arrays.items()}], core_ids=[0])
    return r.results[0]["out_0"].reshape(IMAGES, C, SIDE, SIDE)
```

```python
import numpy as np
from contextlib import ExitStack

import concourse.bass as bass
from concourse import mybir

IMAGES, C, SIDE = 16, 128, 16
PIX = SIDE * SIDE
TOK = IMAGES * PIX
E = 32
K = TOK // E
GROUPS = 8
PER = E // GROUPS
DFF = 341
HH = 32
P = 128
CH = TOK // 512
TPC = 4
TILES = TOK // P
ROW = C + E
FF = [(0, 128), (128, 128), (256, DFF - 256)]
FR = DFF - 256
LEVELS = 5
FLOOR = 2.0 ** -102
EXP_ROUNDS = 7
MAN_ROUNDS = 23

ROUNDS = EXP_ROUNDS + MAN_ROUNDS

C32 = {}
_at = 0
for _n, _w in [("ident", P), ("centre", P), ("two_eye", HH), ("merge", LEVELS * HH), ("merge0", HH), ("tile_start", 1), ("slot_col", 1)]:
    C32[_n] = (_at, _at + _w)
    _at += _w
C32_COLS = _at
C16 = {}
_at = 0
for _n, _w in [("ident", P), ("tri", P), ("slots", P)]:
    C16[_n] = (_at, _at + _w)
    _at += _w
C16_COLS = _at
CH16_COLS = 4 * P

DVE_KEYS = 576
LEAD = 3 * PER
ACT_KEYS = CH * P - DVE_KEYS


def constants():
    i = np.arange(P)
    a = np.zeros((P, C32_COLS), np.float32)
    a[:, slice(*C32["ident"])] = np.eye(P)
    a[:, slice(*C32["centre"])] = np.eye(P) - 1.0 / P
    a[:HH, slice(*C32["two_eye"])] = 2 * np.eye(HH)
    r = np.arange(HH)
    for l in range(LEVELS):
        m = (r[:, None] >> (l + 1) == r[None, :] >> (l + 1)) & ((r[:, None] >> l & 1) == 0) & ((r[None, :] >> l & 1) == 1)
        a[:HH, C32["merge"][0] + l * HH:C32["merge"][0] + (l + 1) * HH] = m.T
        if l == 0:
            a[:HH, slice(*C32["merge0"])] = m
    a[:, C32["tile_start"][0]] = (i % TILES) * P
    a[:, C32["slot_col"][0]] = i
    b = np.zeros((P, C16_COLS), np.float32)
    b[:, slice(*C16["ident"])] = np.eye(P)
    b[:, slice(*C16["tri"])] = i[:, None] <= i[None, :]
    b[:, slice(*C16["slots"])] = i[None, :]
    h = np.zeros((P, CH16_COLS), np.float16)
    u, e = i // E, i % E
    h[:, 0:P] = e[:, None] == e[None, :]
    h[:, P:2 * P] = (e[:, None] == e[None, :]) & (u[:, None] < u[None, :])
    q, t = i // TILES, i % TILES
    h[:, 2 * P:3 * P] = (q[:, None] == q[None, :]) & (t[:, None] < t[None, :])
    h[:, 3 * P:] = -0.5 * (e[:, None] == e[None, :])
    return a, b.astype(np.float16), h


def metaformer_block(nc, x, V, w_router, b_router, w_up, b_up, w_down, b_down, c32, c16, ch16, out):
    f32, f16, i32 = mybir.dt.float32, mybir.dt.float16, mybir.dt.int32
    ALU, ACT, AX = mybir.AluOpType, mybir.ActivationFunctionType, mybir.AxisListType

    rows = nc.dram_tensor("token_rows", (TOK, ROW), f32, kind="Internal").ap()
    acc = [nc.dram_tensor(f"acc{i}", (TOK, C), f32, kind="Internal").ap() for i in range(2)]

    ctx = ExitStack()
    with ctx:
        def sb(name, shape, dt=f32):
            return ctx.enter_context(nc.sbuf_tensor(name, shape, dt))

        def pb(name, shape, dt=f32):
            return ctx.enter_context(nc.psum_tensor(name, shape, dt))

        def sem(name):
            return ctx.enter_context(nc.semaphore(name))

        k32 = sb("k32", [P, C32_COLS])
        k16 = sb("k16", [P, C16_COLS], f16)
        kh16 = sb("kh16", [P, CH16_COLS], f16)

        def c_(name, n=P):
            return k32[0:n, slice(*C32[name])]

        ident, centre = c_("ident"), c_("centre")
        ident16 = k16[:, slice(*C16["ident"])]
        tri16 = k16[:, slice(*C16["tri"])]
        slots16 = k16[:, slice(*C16["slots"])]
        same_expert = kh16[:, 0:P]
        earlier_u = kh16[:, P:2 * P]
        earlier_tile = kh16[:, 2 * P:3 * P]
        half_same_expert = kh16[:, 3 * P:4 * P]

        X = sb("X", [P, CH, 512])
        v_raw = sb("v_raw", [HH, C])
        v_n = sb("v_n", [HH, C])
        v_sq = sb("v_sq", [HH, C])
        v_norm = sb("v_norm", [HH, 3])
        v_t = sb("v_t", [P, HH])
        v_c = sb("v_c", [HH, C])
        gm = sb("gm", [HH, LEVELS, HH])
        g0 = sb("g0", [HH, HH])
        Tm = sb("Tm", [HH, HH])
        Tt = sb("Tt", [HH, HH])
        Am = sb("Am", [HH, HH])
        v_vb = sb("v_vb", [HH, C + E])
        t_vb = sb("t_vb", [HH, C + E])
        cb = sb("cb", [P, C + E])
        warm = sb("warm", [1, 2])
        router = sb("router", [P, E])
        router_b = sb("router_b", [P, E])
        stage_w = sb("stage_w", [P, C + 2 * E])
        bn1 = sb("bn1", [P, CH, TPC, 6])
        mv1 = sb("mv1", [P, CH, TPC, 2])
        ve1 = sb("ve1", [P, CH, TPC])
        rs1 = sb("rs1", [P, CH, TPC])
        bn2 = sb("bn2", [P, CH, TPC, 6])
        mv2 = sb("mv2", [P, CH, TPC, 2])
        ve2 = sb("ve2", [P, CH, TPC])
        rs2 = sb("rs2", [P, CH, TPC])
        nb2 = sb("nb2", [P, CH, TPC])
        mhalf = sb("mhalf", [P, TPC])
        x1 = sb("x1", [P, TILES, C])
        xf = sb("xf", [P, TILES, C])
        mx = sb("mx", [P, CH, TPC])
        sm = sb("sm", [P, CH, TPC])
        rsm = sb("rsm", [P, CH, TPC])
        S = sb("S", [P, TILES, E])
        key = sb("key", [P, CH, P])
        junk = sb("junk", [P, DVE_KEYS], f16)
        junk_a = sb("junk_a", [P, ACT_KEYS], f16)
        cnt_a = sb("cnt_a", [P, 1], f16)
        keys2 = key[:, :, :].rearrange("p g n -> p (g n)")
        cand = sb("cand", [P, 1])
        above = sb("above", [P, 1])
        step = sb("step", [P, 1])
        hit = sb("hit", [P, 1])
        cnt = sb("cnt", [P, 1], f16)
        gt = sb("gt", [P, CH * P], f16)
        eq = sb("eq", [P, CH * P], f16)
        rank = sb("rank", [P, CH * P], f16)
        tie_tot = sb("tie_tot", [P, 1], f16)
        lim = sb("lim", [P, 1])
        tie_ok = sb("tie_ok", [P, CH * P], f16)
        sel = sb("sel", [P, CH * P], f16)
        selT = sb("selT", [P, E, TILES], f16)
        selT_v = selT[:, :, :].rearrange("p e (u g) -> p g u e", u=TPC)
        tot = sb("tot", [P, GROUPS], f16)
        base = sb("base", [P, GROUPS])
        bend = sb("bend", [P, GROUPS])
        cum = sb("cum", [P, GROUPS, P + 2], f16)
        after = sb("after", [P, GROUPS, P], f16)
        onehot = sb("onehot", [P, GROUPS, P], f16)
        junk2 = sb("junk2", [P, P], f16)
        below = sb("below", [P, E])
        idx = sb("idx", [P, E], i32)
        wup = sb("wup", [P, GROUPS, DFF])
        bup = sb("bup", [P, 3, GROUPS])
        wdn = sb("wdn", [P, E, 2, C])
        wdn2 = sb("wdn2", [FR + 1, E, C])
        xg = sb("xg", [P, E, ROW])
        xgT = sb("xgT", [P, 2, 512])
        act = sb("act", [P, 2, 3, 512])
        eo = X[:, :, :].rearrange("p g (q c) -> p (g q) c", c=C)
        zero = sb("zero", [P, 1024])
        xT = xg[:, :, :].rearrange("p e c -> p (e c)")[:, 0:TOK].rearrange("p (g u c) -> p g u c", g=CH, u=TPC)
        lg = act[:, 0, :, :].rearrange("p j n -> p (j n)")[:, 0:CH * P].rearrange("p (g u e) -> p g u e", g=CH, u=TPC)
        pr = act[:, 1, :, :].rearrange("p j n -> p (j n)")[:, 0:CH * P].rearrange("p (g u e) -> p g u e", g=CH, u=TPC)
        y0, y1, ysum, yo = x1, xf, x1, X

        PZ = pb("PZ", [P, 4, 512])
        PT = pb("PT", [P, 2, 512])
        PM = pb("PM", [P, 2, 512])

        s_const = sem("constants_loaded")
        s_const16 = sem("counting_constants_loaded")
        s_v = sem("v_loaded")
        s_router = sem("router_loaded")
        s_x = [sem(f"x_loaded{g}") for g in range(CH)]
        s_wup = sem("w_up_loaded")
        s_wdn = sem("w_down_loaded")
        s_bup = sem("b_up_loaded")
        s_zero = sem("zero_ready")
        s_set = sem("w_setup_pe")
        s_setv = sem("w_setup_dve")
        s_seta = sem("w_setup_act")
        s_fill = sem("fills_ready")
        s_wst = sem("stage_w_ready")
        s_vsq = sem("v_square_sums_ready")
        s_cand = sem("candidate_ready")
        s_cnta = sem("sign_sums_ready")
        s_bias = sem("logits_biased")
        s_smr = sem("softmax_scale_ready")
        s_selp2 = sem("selection_copied_by_act")
        s_cuma = sem("prefix_counts_of_act_ready")
        dch = sem("dve_chain")
        ach = sem("act_chain")
        pch = sem("pool_chain")
        s_xt = sem("x_transposed")
        s_xts = sem("x_transposed_in_sbuf")
        s_z = sem("mixed_ready")
        s_st1 = sem("channel_stats_ready")
        s_rs1 = sem("channel_rstd_ready")
        s_x1 = sem("residual_ready")
        s_st2 = sem("token_stats_ready")
        s_rs2 = sem("token_rstd_ready")
        s_xf = sem("normalised_ready")
        s_zfree = sem("mixed_used")
        s_lg = sem("logits_ready")
        s_exp = sem("exp_ready")
        s_S = sem("softmax_ready")
        s_sT = sem("softmax_transposed")
        s_key = sem("keys_ready")
        s_rows_x = sem("rows_x_stored")
        s_rows_s = sem("rows_s_stored")
        s_acc0 = sem("acc0_filled")
        s_acc1 = sem("acc1_filled")
        s_cnt = sem("counts_ready")
        s_sum = sem("count_sums_ready")
        s_tie = sem("tie_totals_ready")
        s_tieb = sem("tie_bases_ready")
        s_sel = sem("selection_ready")
        s_selp = sem("selection_transposed")
        s_selT = sem("selection_transposed_in_sbuf")
        s_cum = sem("prefix_counts_ready")
        s_tot = sem("tile_totals_ready")
        s_base = sem("tile_bases_ready")
        s_oh = sem("onehot_ready")
        s_find = sem("slot_rows_ready")
        s_idx = sem("indices_ready")
        s_g = [sem(f"gathered{g}") for g in range(GROUPS)]
        s_gT = sem("gathered_transposed")
        s_gTs = sem("gathered_transposed_in_sbuf")
        s_up = sem("up_ready")
        s_act = sem("activated")
        s_dn = sem("down_ready")
        s_eo = sem("expert_out_ready")
        s_sc = [sem(f"scattered{i}") for i in range(2)]
        s_y = [sem(f"y_loaded{g}") for g in range(CH)]
        s_ys = sem("y_summed")
        s_yT = sem("y_transposed")
        s_yo = sem("y_out_ready")
        s_out = sem("out_stored")

        block = ctx.enter_context(nc.Block())

        x_v = x.rearrange("(u k) c (h n) -> k h c u n", k=PIX // 64, h=2)
        out_v = out.rearrange("(u k) c (h n) -> k h c u n", k=PIX // 64, h=2)
        rows_v = rows.rearrange("(u g p) c -> g p u c", u=TPC, p=P)
        acc_v = [a.rearrange("(u g p) c -> g p u c", u=TPC, p=P) for a in acc]

        def b4(t):
            return t.unsqueeze(2).to_broadcast([P, TPC, E])

        def per_chunk(t, g):
            return t[:, g * TPC:(g + 1) * TPC, :]

        @block.sync
        def _(sp):
            sp.dma_start(v_raw[:, :], V).then_inc(s_v, 16)
            sp.dma_start(k32[:, :], c32).then_inc(s_const, 16)
            for g in range(CH):
                sp.dma_start(X[:, g, :].rearrange("p (u n) -> p u n", u=TPC), x_v[g // 2, g % 2]).then_inc(s_x[g], 16)
            sp.dma_start(k16[:, :], c16).then_inc(s_const16, 16)
            sp.dma_start(kh16[:, :], ch16).then_inc(s_const16, 16)
            sp.dma_start(wup[:, :, :], w_up.rearrange("g c f -> c g f")).then_inc(s_wup, 16)
            for j, (f0, fn) in enumerate(FF):
                sp.dma_start(bup[0:fn, j, :], b_up[f0:f0 + fn, :]).then_inc(s_bup, 16)
            for j in range(2):
                sp.dma_start(wdn[:, :, j, :], w_down[:, j * P:(j + 1) * P, :].rearrange("e f c -> f e c")).then_inc(s_wdn, 16)
            sp.dma_start(wdn2[0:FR, :, :], w_down[:, 2 * P:DFF, :].rearrange("e f c -> f e c")).then_inc(s_wdn, 16)
            sp.dma_start(wdn2[FR:FR + 1, :, :], b_down.rearrange("(o e) c -> o e c", o=1)).then_inc(s_wdn, 16)
            sp.wait_ge(s_zero, 1)
            for q in range(4):
                sp.dma_start(acc[1][q * 1024:(q + 1) * 1024, :].rearrange("(p k) c -> p (k c)", p=P), zero[:, :]).then_inc(s_acc1, 16)
            for g in range(CH + 2):
                if g < CH:
                    sp.wait_ge(s_x1, TPC * (g + 1))
                    sp.dma_start(acc_v[0][g], per_chunk(x1, g)).then_inc(s_acc0, 16)
                    sp.wait_ge(s_xf, TPC * (g + 1))
                    sp.dma_start(rows_v[g, :, :, 0:C], per_chunk(xf, g)).then_inc(s_rows_x, 16)
                if g >= 2:
                    sp.wait_ge(s_S, g - 1)
                    sp.dma_start(rows_v[g - 2, :, :, C:ROW], per_chunk(S, g - 2)).then_inc(s_rows_s, 16)
            for i in range(2):
                sp.wait_ge(s_sc[i], 16 * (E // 2))
            for g in range(CH):
                sp.dma_start(per_chunk(y0, g), acc_v[0][g]).then_inc(s_y[g], 16)
                if g == 0:
                    sp.wait_ge(s_rows_x, 16 * CH)
                sp.dma_start(per_chunk(y1, g), acc_v[1][g]).then_inc(s_y[g], 16)
            for g in range(CH):
                sp.wait_ge(s_yo, g + 1)
                sp.dma_start(out_v[g // 2, g % 2], yo[:, g, :].rearrange("p (u n) -> p u n", u=TPC)).then_inc(s_out, 16)
            sp.wait_ge(s_out, 16 * CH)

        @block.gpsimd
        def _(pool):
            nch = [0]

            def link(ins):
                nch[0] += 1
                ins.then_inc(pch, 1)
                pool.wait_ge(pch, nch[0])

            link(nc.gpsimd.memset(mhalf[:, :], -0.5))
            nc.gpsimd.memset(zero[:, :], 0.0).then_inc(s_zero, 1)
            for g in range(CH):
                pool.wait_ge(s_st1, 2 * (g + 1))
                link(nc.gpsimd.tensor_scalar(ve1[:, g, :], mv1[:, g, :, 1], 1e-6, None, ALU.add))
                nc.gpsimd.tensor_tensor(rs1[:, g, :], ve1[:, g, :], mhalf[:, :], ALU.pow).then_inc(s_rs1, 1)
            for g in range(CH + 2):
                if g < CH:
                    pool.wait_ge(s_st2, g + 1)
                    link(nc.gpsimd.tensor_scalar(ve2[:, g, :], mv2[:, g, :, 1], 1e-5, None, ALU.add))
                    link(nc.gpsimd.tensor_tensor(rs2[:, g, :], ve2[:, g, :], mhalf[:, :], ALU.pow))
                    link(nc.gpsimd.tensor_tensor(nb2[:, g, :], mv2[:, g, :, 0], rs2[:, g, :], ALU.mult))
                    nc.gpsimd.tensor_scalar(nb2[:, g, :], nb2[:, g, :], -1.0, None, ALU.mult).then_inc(s_rs2, 1)
                    pool.wait_ge(s_zfree, g + 1)
                    L = lg[:, g, :, :]
                    link(nc.gpsimd.tensor_tensor(L, L, b4(rs2[:, g, :]), ALU.mult))
                    if g == 0:
                        pool.wait_ge(s_router, 32)
                    nc.gpsimd.tensor_tensor(L, L, router_b[:, :].unsqueeze(1).to_broadcast([P, TPC, E]), ALU.add).then_inc(s_bias, 1)
                if g >= 2:
                    pool.wait_ge(s_smr, g - 1)
                    nc.gpsimd.tensor_tensor(per_chunk(S, g - 2), pr[:, g - 2, :, :], b4(rsm[:, g - 2, :]), ALU.mult).then_inc(s_S, 1)
            pool.wait_ge(s_S, CH)
            nc.gpsimd.memset(act[64:P, :, 2, :], 1.0).then_inc(s_fill, 1)

            def gather(e):
                pool.wait_ge(s_idx, e + 1)
                nc.gpsimd.indirect_dma_start(
                    out=xg[:, e, :], out_offset=None, in_=rows[:, :],
                    in_offset=bass.IndirectOffsetOnAxis(ap=idx[:, e:e + 1], axis=0)).then_inc(s_g[e // PER], 16)

            def scatter(e):
                pool.wait_ge(s_eo, e + 1)
                if e >= 2:
                    pool.wait_ge(s_sc[e % 2], 16 * (e // 2))
                nc.gpsimd.indirect_dma_start(
                    out=acc[e % 2][:, :], out_offset=bass.IndirectOffsetOnAxis(ap=idx[:, e:e + 1], axis=0),
                    in_=eo[:, e, :], in_offset=None, compute_op=ALU.add).then_inc(s_sc[e % 2], 16)

            pool.wait_ge(s_rows_x, 16 * CH)
            pool.wait_ge(s_rows_s, 16 * CH)
            pool.wait_ge(s_acc0, 16 * CH)
            pool.wait_ge(s_acc1, 16 * 4)
            for e in range(E + LEAD):
                if e < E:
                    gather(e)
                if e >= LEAD:
                    scatter(e - LEAD)

        @block.scalar
        def _(a):
            nch = [0]

            def link(ins):
                nch[0] += 1
                ins.then_inc(ach, 1)
                a.wait_ge(ach, nch[0])

            a.dma_start(router[:, :], w_router).then_inc(s_router, 16)
            a.dma_start(router_b[:, :], b_router.rearrange("(o e) -> o e", o=1).to_broadcast([P, E])).then_inc(s_router, 16)
            a.wait_ge(s_vsq, 1)
            nc.scalar.activation(v_norm[:, 1:2], v_norm[:, 0:1], ACT.Sqrt).then_inc(s_seta, 1)

            def copy_x(g):
                a.wait_ge(s_xt, g + 1)
                nc.scalar.activation(xT[:, g, :, :], PT[:, g % 2, :].rearrange("p (u c) -> p u c", u=TPC), ACT.Copy).then_inc(s_xts, 1)

            def normalise(g):
                a.wait_ge(s_rs2, g + 1)
                for u in range(TPC):
                    nc.scalar.activation(xf[:, g * TPC + u, :], x1[:, g * TPC + u, :], ACT.Identity,
                                         bias=nb2[:, g, u:u + 1], scale=rs2[:, g, u:u + 1]).then_inc(s_xf, 1)

            def exps(g):
                a.wait_ge(s_lg, g + 1)
                nc.scalar.activation(pr[:, g, :, :], lg[:, g, :, :], ACT.Exp).then_inc(s_exp, 1)

            for g in range(CH):
                copy_x(g)
            for g in range(CH + 1):
                if g < CH:
                    normalise(g)
                if g >= 1:
                    exps(g - 1)

            a.wait_ge(s_key, CH)
            for j in range(ROUNDS):
                a.wait_ge(s_cand, j + 1)
                with nc.allow_low_precision(reason="a sum of at most ACT_KEYS signs is exact in float16"):
                    nc.scalar.activation(junk_a[:, :], keys2[:, DVE_KEYS:CH * P], ACT.Sign, bias=cand[:, 0:1], scale=-1.0,
                                         accum_out=cnt_a[:, 0:1]).then_inc(s_cnta, 1)
            a.wait_ge(s_selp, 2)
            nc.scalar.activation(selT_v[:, CH // 2:CH, :, :], PT[:, 1, 0:256].bitcast(f16).rearrange("p (g u e) -> p g u e", g=CH // 2, u=TPC),
                                 ACT.Copy).then_inc(s_selp2, 1)
            a.wait_ge(s_base, 2)
            for g in range(GROUPS // 2, GROUPS):
                nc.scalar.activation(cum[:, g, 0:P], PZ[:, 1, (g - GROUPS // 2) * P:(g - GROUPS // 2 + 1) * P], ACT.Identity,
                                     bias=base[:, g:g + 1]).then_inc(s_cuma, 1)
            for g in range(GROUPS):
                a.wait_ge(s_gT, g + 1)
                if g >= 2:
                    a.wait_ge(s_up, 3 * (g - 1))
                nc.scalar.activation(xgT[:, g % 2, :], PT[:, 0, :], ACT.Copy).then_inc(s_gTs, 1)
                if g == 0:
                    a.wait_ge(s_bup, 48)
                    a.wait_ge(s_fill, 1)
                for j, (f0, fn) in enumerate(FF):
                    a.wait_ge(s_up, 3 * g + j + 1)
                    if g >= 2 and j == 0:
                        a.wait_ge(s_dn, PER * (g - 1))
                    src = PT[0:fn, 1, :] if (3 * g + j) % 2 == 0 else PM[0:fn, 0, :]
                    nc.scalar.activation(act[0:fn, g % 2, j, :], src, ACT.Silu, bias=bup[0:fn, j, g:g + 1]).then_inc(s_act, 1)
            for g in range(CH):
                a.wait_ge(s_yT, g + 1)
                nc.scalar.activation(yo[:, g, :], PT[:, g % 2, :], ACT.Copy).then_inc(s_yo, 1)

        @block.vector
        def _(v):
            nch = [0]

            def link(ins):
                nch[0] += 1
                ins.then_inc(dch, 1)
                v.wait_ge(dch, nch[0])

            halves = []

            def stats1():
                n = len(halves)
                if n:
                    g, u0, at = halves[-1]
                    v.wait_ge(dch, at)
                    for u in (u0, u0 + 1):
                        ins = nc.vector.bn_aggr(mv1[:, g, u, :], bn1[:, g, u, :])
                    ins.then_inc(s_st1, 1)
                if n < 2 * CH:
                    g, u0 = n // 2, 2 * (n % 2)
                    v.wait_ge(s_xts, g + 1)
                    for u in (u0, u0 + 1):
                        ins = nc.vector.bn_stats(bn1[:, g, u, :], xT[:, g, u, :])
                    nch[0] += 1
                    ins.then_inc(dch, 1)
                    halves.append((g, u0, nch[0]))

            v.wait_ge(s_v, 16)
            nc.vector.scalar_tensor_tensor(v_sq[:, :], v_raw[:, :], 1.0, v_raw[:, :], ALU.mult, ALU.mult, accum_out=v_norm[:, 0:1]).then_inc(s_vsq, 1)
            v.wait_ge(s_const, 16)
            nc.vector.tensor_copy(cb[:, 0:C], centre)
            v.wait_ge(s_set, 1)
            nc.vector.tensor_copy(cb[:, C:C + E], PM[:, 1, 0:E])
            nc.vector.tensor_copy(stage_w[:, C + E:C + 2 * E], PM[:, 1, 0:E]).then_inc(s_setv, 1)
            v.wait_ge(s_seta, 1)
            link(nc.vector.tensor_scalar(v_norm[:, 1:2], v_norm[:, 1:2], 1e-8, None, ALU.add))
            link(nc.vector.reciprocal(v_norm[:, 2:3], v_norm[:, 1:2]))
            nc.vector.tensor_scalar(v_vb[:, 0:C], v_raw[:, :], v_norm[:, 2:3], None, ALU.mult).then_inc(s_setv, 1)
            v.wait_ge(s_set, 2)
            nc.vector.tensor_copy(v_t[:, :], PM[:, 0, 0:HH]).then_inc(s_setv, 1)
            stats1()
            v.wait_ge(s_set, 3)
            link(nc.vector.tensor_tensor(gm[:, :, :], PM[0:HH, 1, 0:HH].unsqueeze(1).to_broadcast([HH, LEVELS, HH]),
                                         c_("merge", HH).rearrange("p (l h) -> p l h", l=LEVELS), ALU.mult))
            link(nc.vector.tensor_tensor(g0[:, :], PM[0:HH, 1, 0:HH], c_("merge0", HH), ALU.mult))
            nc.vector.scalar_tensor_tensor(Tt[:, :], gm[:, 0, :], -4.0, c_("two_eye", HH), ALU.mult, ALU.add)
            nc.vector.scalar_tensor_tensor(Tm[:, :], g0[:, :], -4.0, c_("two_eye", HH), ALU.mult, ALU.add).then_inc(s_setv, 1)
            stats1()
            v.wait_ge(s_set, 4)
            nc.vector.tensor_copy(v_c[:, :], PM[0:HH, 0, 0:C])
            nc.vector.tensor_copy(v_vb[:, C:C + E], PM[0:HH, 0, C:C + E]).then_inc(s_setv, 1)
            for l in range(1, LEVELS):
                stats1()
                v.wait_ge(s_set, 3 + 2 * l)
                nc.vector.tensor_copy(Am[:, :], PM[0:HH, 0, 0:HH]).then_inc(s_setv, 1)
                stats1()
                v.wait_ge(s_set, 4 + 2 * l)
                nc.vector.tensor_tensor(Tm[:, :], Tm[:, :], PM[0:HH, 1, 0:HH], ALU.subtract)
                nc.vector.tensor_tensor(Tt[:, :], Tt[:, :], PM[0:HH, 1, HH:2 * HH], ALU.subtract).then_inc(s_setv, 1)
            n = 2 + 2 * LEVELS
            stats1()
            v.wait_ge(s_set, n + 1)
            nc.vector.tensor_copy(t_vb[:, :], PM[0:HH, 0, 0:C + E]).then_inc(s_setv, 1)
            stats1()
            v.wait_ge(s_set, n + 2)
            nc.vector.tensor_tensor(stage_w[:, 0:C + E], cb[:, :], PM[:, 1, 0:C + E], ALU.subtract).then_inc(s_wst, 1)
            while len(halves) < 2 * CH:
                stats1()
            stats1()

            def zview(g, lo, n):
                return PZ[:, 2 * (g % 2):2 * (g % 2) + 2, 0:2 * (C + 2 * E)].rearrange("p k (w c) -> p k w c", w=2)[:, :, :, lo:lo + n]

            def residual(g):
                v.wait_ge(s_z, g + 1)
                v.wait_ge(s_rs1, g + 1)
                for u in range(TPC):
                    z = PZ[:, 2 * (g % 2) + u // 2, (u % 2) * (C + 2 * E):(u % 2) * (C + 2 * E) + C]
                    nc.vector.scalar_tensor_tensor(x1[:, g * TPC + u, :], z, rs1[:, g, u:u + 1], xT[:, g, u, :],
                                                   ALU.mult, ALU.add).then_inc(s_x1, 1)

            def stats2(g):
                v.wait_ge(s_x1, TPC * (g + 1))
                for u in range(TPC):
                    ins = nc.vector.bn_stats(bn2[:, g, u, :], x1[:, g * TPC + u, :])
                link(ins)
                for u in range(TPC):
                    ins = nc.vector.bn_aggr(mv2[:, g, u, :], bn2[:, g, u, :])
                ins.then_inc(s_st2, 1)

            def b22(t):
                return t.rearrange("p (k w) -> p k w", k=2).unsqueeze(3).to_broadcast([P, 2, 2, E])

            def logits(g):
                L22 = lg[:, g, :, :].rearrange("p (k w) e -> p k w e", k=2)
                ins = nc.vector.tensor_tensor(L22, zview(g, C, E), b22(rs1[:, g, :]), ALU.mult)
                nch[0] += 1
                ins.then_inc(dch, 1)
                return nch[0]

            def logits_sum(g, at):
                L22 = lg[:, g, :, :].rearrange("p (k w) e -> p k w e", k=2)
                v.wait_ge(dch, at)
                nc.vector.tensor_tensor(L22, L22, zview(g, C + E, E), ALU.add).then_inc(s_zfree, 1)

            def less_max(g):
                v.wait_ge(s_bias, g + 1)
                link(nc.vector.tensor_reduce(mx[:, g, :], lg[:, g, :, :], AX.X, ALU.max))
                nc.vector.tensor_tensor(lg[:, g, :, :], lg[:, g, :, :], b4(mx[:, g, :]), ALU.subtract).then_inc(s_lg, 1)

            def softmax_scale(g):
                v.wait_ge(s_exp, g + 1)
                link(nc.vector.tensor_reduce(sm[:, g, :], pr[:, g, :, :], AX.X, ALU.add))
                nc.vector.reciprocal(rsm[:, g, :], sm[:, g, :]).then_inc(s_smr, 1)

            def keys(g):
                v.wait_ge(s_sT, g + 1)
                nc.vector.tensor_scalar(key[:, g, :], PM[:, g % 2, 0:P], FLOOR, None, ALU.max).then_inc(s_key, 1)

            for g in range(CH + 3):
                if g < CH:
                    residual(g)
                    at = logits(g)
                    stats2(g)
                    logits_sum(g, at)
                if g >= 3:
                    keys(g - 3)
                if 1 <= g <= CH:
                    less_max(g - 1)
                if 2 <= g <= CH + 1:
                    softmax_scale(g - 2)

            v.wait_ge(s_key, CH)
            nc.vector.memset(cand[:, :], FLOOR * 2.0 ** 64).then_inc(s_cand, 1)
            REACHED = float(K - 2 * ACT_KEYS)

            def count(j):
                v.wait_ge(s_cand, j + 1)
                nc.vector.tensor_scalar(junk[:, :], keys2[:, 0:DVE_KEYS], cand[:, 0:1], None, ALU.is_ge, ALU.add, accum_out=cnt[:, 0:1]).then_inc(s_cnt, 1)
                v.wait_ge(s_sum, j + 1)

            for j in range(EXP_ROUNDS):
                count(j)
                last = j == EXP_ROUNDS - 1
                f = 1.0 if last else 2.0 ** (2 ** (EXP_ROUNDS - 2 - j))
                inv = 0.5 if last else 1.0 / f
                link(nc.vector.tensor_scalar(hit[:, :], PM[:, 0, 0:1], REACHED, float(np.float32(f - inv)), ALU.is_ge, ALU.mult))
                ins = nc.vector.scalar_tensor_tensor(cand[:, :], hit[:, :], inv, cand[:, :], ALU.add, ALU.mult)
                if last:
                    link(ins)
                else:
                    ins.then_inc(s_cand, 1)
            nc.vector.tensor_scalar(step[:, :], cand[:, :], 0.5, None, ALU.mult).then_inc(dch, 1)
            nc.vector.tensor_scalar(cand[:, :], cand[:, :], 1.5, None, ALU.mult).then_inc(s_cand, 1)
            nch[0] += 1
            for j in range(EXP_ROUNDS, ROUNDS):
                count(j)
                last = j == ROUNDS - 1
                link(nc.vector.tensor_scalar(hit[:, :], PM[:, 0, 0:1], REACHED, 1.0 if last else 0.5, ALU.is_ge, ALU.subtract))
                nc.vector.scalar_tensor_tensor(cand[:, :], hit[:, :], step[:, 0:1], cand[:, :], ALU.mult, ALU.add).then_inc(s_cand, 1)
                if not last:
                    nc.vector.tensor_scalar(step[:, :], step[:, :], 0.5, None, ALU.mult).then_inc(dch, 1)
                    nch[0] += 1
            v.wait_ge(s_cand, ROUNDS + 1)
            link(nc.vector.tensor_tensor(above[:, :], cand[:, :], step[:, :], ALU.add))
            nc.vector.tensor_scalar(gt[:, :], keys2, above[:, 0:1], None, ALU.is_ge, ALU.add, accum_out=cnt[:, 0:1]).then_inc(s_cnt, 1)
            v.wait_ge(s_sum, ROUNDS + 1)
            link(nc.vector.tensor_scalar(hit[:, :], PM[:, 0, 0:1], float(K), None, ALU.is_ge))
            link(nc.vector.scalar_tensor_tensor(cand[:, :], hit[:, :], step[:, 0:1], cand[:, :], ALU.mult, ALU.add))

            nc.vector.tensor_scalar(gt[:, :], keys2, cand[:, 0:1], None, ALU.is_gt, ALU.add, accum_out=cnt[:, 0:1]).then_inc(s_cnt, 1)
            link(nc.vector.tensor_scalar(eq[:, :], keys2, cand[:, 0:1], None, ALU.is_equal))
            link(nc.vector.tensor_tensor_scan(rank[:, :], eq[:, :], eq[:, :], 0.0, ALU.add, ALU.max))
            nc.vector.tensor_copy(tie_tot[:, :], rank[:, CH * P - 1:CH * P]).then_inc(s_tie, 1)
            v.wait_ge(s_tieb, 1)
            link(nc.vector.tensor_scalar(lim[:, :], PM[:, 1, 0:1], -1.0, float(K), ALU.mult, ALU.add))
            for h in range(2):
                o = slice(h * CH * P // 2, (h + 1) * CH * P // 2)
                link(nc.vector.scalar_tensor_tensor(tie_ok[:, o], rank[:, o], lim[:, 0:1], eq[:, o], ALU.is_le, ALU.mult))
                nc.vector.tensor_tensor(sel[:, o], gt[:, o], tie_ok[:, o], ALU.add).then_inc(s_sel, 1)
            v.wait_ge(s_selp, 1)
            nc.vector.tensor_copy(selT_v[:, 0:CH // 2, :, :], PT[:, 0, 0:256].bitcast(f16).rearrange("p (g u e) -> p g u e", g=CH // 2, u=TPC)).then_inc(s_selT, 1)

            v.wait_ge(s_cum, 1)
            link(nc.vector.tensor_copy(tot[:, :], PZ[:, 0:2, :].rearrange("p k (g n) -> p (k g) n", n=P)[:, :, P - 1]))
            nc.vector.tensor_copy(cum[:, :, P:P + 1], c_("tile_start").unsqueeze(1).to_broadcast([P, GROUPS, 1])).then_inc(s_tot, 1)
            v.wait_ge(s_base, 1)
            ins = nc.vector.tensor_copy(base[:, :], PM[:, 1, 0:GROUPS])
            ins.then_inc(s_base, 1)
            v.wait_ge(s_base, 2)
            nc.vector.tensor_tensor(bend[:, :], base[:, :], tot[:, :], ALU.add)
            link(nc.vector.tensor_tensor(cum[:, 0:GROUPS // 2, 0:P], PZ[:, 0, :].rearrange("p (g n) -> p g n", n=P),
                                         base[:, 0:GROUPS // 2].unsqueeze(2).to_broadcast([P, GROUPS // 2, P]), ALU.add))

            def one_hot(g):
                link(nc.vector.tensor_scalar(after[:, g, :], slots16, base[:, g:g + 1], None, ALU.is_ge))
                nc.vector.scalar_tensor_tensor(onehot[:, g, :], slots16, bend[:, g:g + 1], after[:, g, :], ALU.is_lt, ALU.mult).then_inc(s_oh, 1)

            one_hot(0)
            one_hot(1)
            for g in range(GROUPS):
                for e in range(g * PER, (g + 1) * PER):
                    v.wait_ge(s_find, e + 1)
                    link(nc.vector.tensor_scalar(junk2[:, :], PZ[:, e % PER, 0:P], c_("slot_col"), None, ALU.is_le, ALU.add,
                                                 accum_out=below[:, e:e + 1]))
                    nc.vector.tensor_tensor(idx[:, e:e + 1], below[:, e:e + 1], PZ[:, e % PER, P:P + 1], ALU.add).then_inc(s_idx, 1)
                if g + 2 < GROUPS:
                    one_hot(g + 2)

            for e in range(E):
                v.wait_ge(s_dn, e + 1)
                nc.vector.tensor_scalar(eo[:, e, :], PZ[:, e % PER, 0:C], xg[:, e, C + e:C + e + 1], None, ALU.mult).then_inc(s_eo, 1)
            for g in range(CH):
                v.wait_ge(s_y[g], 32)
                nc.vector.tensor_tensor(per_chunk(ysum, g), per_chunk(y0, g), per_chunk(y1, g), ALU.add).then_inc(s_ys, 1)

        @block.tensor
        def _(pe):
            mm = nc.tensor.matmul
            def x_transpose(g):
                pe.wait_ge(s_x[g], 16)
                if g >= 2:
                    pe.wait_ge(s_xts, g - 1)
                for u in range(TPC):
                    ins = nc.tensor.transpose(PT[:, g % 2, u * P:(u + 1) * P], X[:, g, u * P:(u + 1) * P], ident)
                ins.then_inc(s_xt, 1)

            pe.wait_ge(s_const, 16)
            pe.wait_ge(s_router, 32)
            v_n = v_vb[:, 0:C]
            mm(PM[:, 1, 0:E], centre, router[:, :], start=True, stop=True).then_inc(s_set, 1)
            x_transpose(0)
            pe.wait_ge(s_setv, 2)
            nc.tensor.transpose(PM[:, 0, 0:HH], v_n, c_("ident", HH)[:, 0:HH]).then_inc(s_set, 1)
            pe.wait_ge(s_setv, 3)
            mm(PM[0:HH, 1, 0:HH], v_t[:, :], v_t[:, :], start=True, stop=True).then_inc(s_set, 1)
            mm(PM[0:HH, 0, 0:C + E], v_t[:, :], cb[:, :], start=True, stop=True).then_inc(s_set, 1)
            x_transpose(1)
            pe.wait_ge(s_setv, 5)
            for l in range(1, LEVELS):
                mm(PM[0:HH, 0, 0:HH], gm[:, l, :], Tm[:, :], start=True, stop=True).then_inc(s_set, 1)
                pe.wait_ge(s_setv, 4 + 2 * l)
                mm(PM[0:HH, 1, 0:HH], Tt[:, :], Am[:, :], start=True, stop=True)
                mm(PM[0:HH, 1, HH:2 * HH], Am[:, :], Tt[:, :], start=True, stop=True).then_inc(s_set, 1)
                x_transpose(l + 1)
                pe.wait_ge(s_setv, 5 + 2 * l)
            n = 3 + 2 * LEVELS
            mm(PM[0:HH, 0, 0:C + E], Tt[:, :], v_vb[:, :], start=True, stop=True).then_inc(s_set, 1)
            x_transpose(LEVELS + 1)
            pe.wait_ge(s_setv, n + 1)
            mm(PM[:, 1, 0:C + E], v_c[:, :], t_vb[:, :], start=True, stop=True).then_inc(s_set, 1)
            x_transpose(LEVELS + 2)

            def keys_transpose(g):
                pe.wait_ge(s_S, g + 1)
                if g >= 2:
                    pe.wait_ge(s_key, g - 1)
                nc.tensor.transpose(PM[:, g % 2, 0:P], per_chunk(S, g).rearrange("p u e -> p (u e)"), ident).then_inc(s_sT, 1)

            pe.wait_ge(s_wst, 1)
            for g in range(CH + 3):
                if g < CH:
                    if g >= 2:
                        pe.wait_ge(s_zfree, g - 1)
                    W_ = C + 2 * E
                    for u in range(TPC):
                        ins = mm(PZ[:, 2 * (g % 2) + u // 2, (u % 2) * W_:(u % 2 + 1) * W_], X[:, g, u * P:(u + 1) * P], stage_w[:, :],
                                 start=True, stop=True)
                    ins.then_inc(s_z, 1)
                if g >= 3:
                    keys_transpose(g - 3)

            pe.wait_ge(s_key, CH)
            pe.wait_ge(s_const16, 32)
            for j in range(ROUNDS):
                pe.wait_ge(s_cnt, j + 1)
                mm(PM[:, 0, 0:1], same_expert, cnt[:, 0:1], start=True, stop=False)
                pe.wait_ge(s_cnta, j + 1)
                mm(PM[:, 0, 0:1], half_same_expert, cnt_a[:, 0:1], start=False, stop=True).then_inc(s_sum, 1)
            pe.wait_ge(s_cnt, ROUNDS + 1)
            mm(PM[:, 0, 0:1], same_expert, cnt[:, 0:1], start=True, stop=True).then_inc(s_sum, 1)
            pe.wait_ge(s_cnt, ROUNDS + 2)
            mm(PM[:, 1, 0:1], same_expert, cnt[:, 0:1], start=True, stop=False)
            pe.wait_ge(s_tie, 1)
            mm(PM[:, 1, 0:1], earlier_u, tie_tot[:, :], start=False, stop=True).then_inc(s_tieb, 1)
            for h in range(2):
                pe.wait_ge(s_sel, h + 1)
                for k in range(CH // 2):
                    g = h * CH // 2 + k
                    ins = nc.tensor.transpose(PT[:, h, 0:256].bitcast(f16)[:, k * P:(k + 1) * P], sel[:, g * P:(g + 1) * P], ident16)
                ins.then_inc(s_selp, 1)
            pe.wait_ge(s_selT, 1)
            pe.wait_ge(s_selp2, 1)
            for g in range(GROUPS):
                ins = mm(PZ[:, g // 4, (g % 4) * P:(g % 4 + 1) * P], selT[:, g * PER:(g + 1) * PER, :].rearrange("p e t -> p (e t)"), tri16,
                         start=True, stop=True)
            ins.then_inc(s_cum, 1)
            pe.wait_ge(s_tot, 1)
            mm(PM[:, 1, 0:GROUPS], earlier_tile, tot[:, :], start=True, stop=True).then_inc(s_base, 1)
            for g in range(GROUPS):
                pe.wait_ge(s_oh, g + 1)
                if g == 0:
                    pe.wait_ge(s_cuma, GROUPS // 2)
                for q in range(PER):
                    if g >= 1:
                        pe.wait_ge(s_idx, (g - 1) * PER + q + 1)
                    r = slice(q * TILES, (q + 1) * TILES)
                    mm(PZ[:, q, 0:P + 1], onehot[r, g, :], cum[r, g, 0:P + 1], start=True, stop=True).then_inc(s_find, 1)

            def gathered_transpose(g):
                pe.wait_ge(s_g[g], 16 * PER)
                if g >= 1:
                    pe.wait_ge(s_gTs, g)
                for q in range(PER):
                    ins = nc.tensor.transpose(PT[:, 0, q * P:(q + 1) * P], xg[:, g * PER + q, 0:C], ident)
                ins.then_inc(s_gT, 1)

            def up(g):
                pe.wait_ge(s_gTs, g + 1)
                for j, (f0, fn) in enumerate(FF):
                    n = 3 * g + j
                    if n >= 2:
                        pe.wait_ge(s_act, n - 1)
                    dst = PT[0:fn, 1, :] if n % 2 == 0 else PM[0:fn, 0, :]
                    mm(dst, wup[:, g, f0:f0 + fn], xgT[:, g % 2, :], start=True, stop=True).then_inc(s_up, 1)

            def down(g):
                pe.wait_ge(s_act, 3 * (g + 1))
                for q in range(PER):
                    e = g * PER + q
                    if g >= 1:
                        pe.wait_ge(s_eo, e - PER + 1)
                    for j in range(3):
                        w = wdn[:, e, j, :] if j < 2 else wdn2[:, e, :]
                        k = P if j < 2 else FR + 1
                        ins = mm(PZ[:, q, 0:C], act[0:k, g % 2, j, q * P:(q + 1) * P], w, start=(j == 0), stop=(j == 2))
                    ins.then_inc(s_dn, 1)

            pe.wait_ge(s_idx, E)
            pe.wait_ge(s_wup, 16)
            pe.wait_ge(s_wdn, 64)
            for g in range(GROUPS + 1):
                if g < GROUPS:
                    gathered_transpose(g)
                    up(g)
                if g >= 1:
                    down(g - 1)
            for g in range(CH):
                pe.wait_ge(s_ys, g + 1)
                if g >= 2:
                    pe.wait_ge(s_yo, g - 1)
                for u in range(TPC):
                    ins = nc.tensor.transpose(PT[:, g % 2, u * P:(u + 1) * P], ysum[:, g * TPC + u, :], ident)
                ins.then_inc(s_yT, 1)


_INS = ["x", "L0_conv_V", "L0_ffn_W_router", "L0_ffn_b_router", "L0_ffn_W_up", "L0_ffn_b_up", "L0_ffn_W_down", "L0_ffn_b_down"]


def kernel(**inputs):
    import concourse.bacc as bacc
    from concourse.bass_utils import run_bass_kernel_spmd as run

    nc = bacc.Bacc("TRN2", target_bir_lowering=False, num_devices=1)
    arrays = {name: np.ascontiguousarray(inputs[name]) for name in _INS}
    arrays["x"] = arrays["x"].reshape(IMAGES, C, PIX)
    arrays["L0_ffn_b_up"] = np.ascontiguousarray(arrays["L0_ffn_b_up"].T)
    arrays.update(zip(("const_f32", "const_f16", "const_counting"), constants()))
    args = [nc.dram_tensor(f"in_{n}", a.shape, mybir.dt.from_np(a.dtype), kind="ExternalInput").ap() for n, a in arrays.items()]
    out = nc.dram_tensor("out_0", (IMAGES, C, PIX), mybir.dt.float32, kind="ExternalOutput").ap()
    metaformer_block(nc, *args, out)
    r = run(nc, [{f"in_{n}": a for n, a in arrays.items()}], core_ids=[0])
    return r.results[0]["out_0"].reshape(IMAGES, C, SIDE, SIDE)
```

```python
import numpy as np
from contextlib import ExitStack

import concourse.bass as bass
from concourse import mybir

IMAGES, C, SIDE = 16, 128, 16
PIX = SIDE * SIDE
TOK = IMAGES * PIX
E = 32
K = TOK // E
GROUPS = 8
PER = E // GROUPS
DFF = 341
HH = 32
P = 128
CH = TOK // 512
TPC = 4
TILES = TOK // P
ROW = C + E
FF = [(0, 128), (128, 128), (256, DFF - 256)]
FR = DFF - 256
LEVELS = HH.bit_length() - 1
FLOOR = 2.0 ** -102
LOW_EXP, EXP_ROUNDS, MAN_ROUNDS = -8, 3, 6
ROUNDS = EXP_ROUNDS + MAN_ROUNDS
FULL_EXP_ROUNDS, FULL_MAN_ROUNDS = 7, 23
QUARTERS = P // E
CANDS = 8 * QUARTERS

C32 = {}
_at = 0
for _n, _w in [("ident", P), ("centre", P), ("two_eye", HH), ("merge", LEVELS * HH), ("merge0", HH), ("tile_start", 1), ("slot_col", 1)]:
    C32[_n] = (_at, _at + _w)
    _at += _w
C32_COLS = _at
C16 = {}
_at = 0
for _n, _w in [("ident", P), ("tri", P), ("slots", P)]:
    C16[_n] = (_at, _at + _w)
    _at += _w
C16_COLS = _at
CH16_COLS = 5 * P + 1

DVE_KEYS = 544
ACT_KEYS = CH * P - DVE_KEYS

XAHEAD = 4
XSLOTS = (3, 2, 2, 2, 1, 1, 1, 1, 1)
ACT_STATS = (2, 3, 4, 5, 6)
DVE_STATS = tuple(g for g in range(CH) if g not in ACT_STATS)
LATE_STATS = 4
SCALE_LAG = 3
KEYS_LAG = 6

LEAD, CLOSING, AHEAD = 15, 0.77, 16
INTO = tuple(e % 2 if e < E - 1 else 0 for e in range(E))
UNIT_SIZES = (4, 4, 4, 4, 4, 4, 4, 2, 2)
UNITS = tuple((sum(UNIT_SIZES[:k]), n) for k, n in enumerate(UNIT_SIZES))
UNIT_OF = tuple(k for k, n in enumerate(UNIT_SIZES) for _ in range(n))
EARLY = range(1, 9)


def constants():
    i = np.arange(P)
    a = np.zeros((P, C32_COLS), np.float32)
    a[:, slice(*C32["ident"])] = np.eye(P)
    a[:, slice(*C32["centre"])] = np.eye(P) - 1.0 / P
    a[:HH, slice(*C32["two_eye"])] = 2 * np.eye(HH)
    r = np.arange(HH)
    for l in range(LEVELS):
        m = (r[:, None] >> (l + 1) == r[None, :] >> (l + 1)) & ((r[:, None] >> l & 1) == 0) & ((r[None, :] >> l & 1) == 1)
        a[:HH, C32["merge"][0] + l * HH:C32["merge"][0] + (l + 1) * HH] = m.T
        if l == 0:
            a[:HH, slice(*C32["merge0"])] = m
    a[:, C32["tile_start"][0]] = (i % TILES) * P
    a[:, C32["slot_col"][0]] = i
    b = np.zeros((P, C16_COLS), np.float32)
    b[:, slice(*C16["ident"])] = np.eye(P)
    b[:, slice(*C16["tri"])] = i[:, None] <= i[None, :]
    b[:, slice(*C16["slots"])] = i[None, :]
    h = np.zeros((P, CH16_COLS), np.float16)
    u, e = i // E, i % E
    h[:, 0:P] = e[:, None] == e[None, :]
    h[:, P:2 * P] = (e[:, None] == e[None, :]) & (u[:, None] < u[None, :])
    q, t = i // TILES, i % TILES
    h[:, 2 * P:3 * P] = (q[:, None] == q[None, :]) & (t[:, None] < t[None, :])
    h[:, 3 * P:4 * P] = 4.0 * (e[:, None] == e[None, :])
    h[:, 4 * P:5 * P] = -2.0 * (e[:, None] == e[None, :])
    h[:, 5 * P] = (8 * ACT_KEYS - 4 * K) // QUARTERS + (u == 0)
    return a, b.astype(np.float16), h


def metaformer_block(nc, x, V, w_router, b_router, w_up, b_up, w_down, b_down, c32, c16, ch16, out):
    f32, f16, i32 = mybir.dt.float32, mybir.dt.float16, mybir.dt.int32
    ALU, ACT, AX = mybir.AluOpType, mybir.ActivationFunctionType, mybir.AxisListType

    rows = nc.dram_tensor("token_rows", (TOK, ROW), f32, kind="Internal").ap()
    acc = [nc.dram_tensor(f"acc{i}", (TOK, C), f32, kind="Internal").ap() for i in range(2)]

    ctx = ExitStack()
    with ctx:
        def sb(name, shape, dt=f32):
            return ctx.enter_context(nc.sbuf_tensor(name, shape, dt))

        def pb(name, shape, dt=f32):
            return ctx.enter_context(nc.psum_tensor(name, shape, dt))

        def sem(name):
            return ctx.enter_context(nc.semaphore(name))

        k32 = sb("k32", [P, C32_COLS])
        k16 = sb("k16", [P, C16_COLS], f16)
        kh16 = sb("kh16", [P, CH16_COLS], f16)

        def c_(name, n=P):
            return k32[0:n, slice(*C32[name])]

        ident, centre = c_("ident"), c_("centre")
        ident16 = k16[:, slice(*C16["ident"])]
        tri16 = k16[:, slice(*C16["tri"])]
        slots16 = k16[:, slice(*C16["slots"])]
        same_expert = kh16[:, 0:P]
        earlier_u = kh16[:, P:2 * P]
        earlier_tile = kh16[:, 2 * P:3 * P]
        same_expert_4 = kh16[:, 3 * P:4 * P]
        same_expert_m2 = kh16[:, 4 * P:5 * P]
        sum_bias = kh16[:, 5 * P:5 * P + 1]

        X = sb("X", [P, CH, 512])
        v_raw = sb("v_raw", [HH, C])
        v_sq = sb("v_sq", [HH, C])
        v_norm = sb("v_norm", [HH, 3])
        v_t = sb("v_t", [P, HH])
        v_c = sb("v_c", [HH, C])
        gm = sb("gm", [HH, LEVELS, HH])
        g0 = sb("g0", [HH, HH])
        Tm = sb("Tm", [HH, HH])
        Tt = sb("Tt", [HH, HH])
        Am = sb("Am", [HH, HH])
        v_vb = sb("v_vb", [HH, C + E])
        t_vb = sb("t_vb", [HH, C + E])
        cb = sb("cb", [P, C + E])
        warm = sb("warm", [1, 2])
        router = sb("router", [P, E])
        router_b = sb("router_b", [P, E])
        stage_w = sb("stage_w", [P, C + 2 * E])
        bn1 = sb("bn1", [P, CH, TPC, 6])
        mv1 = sb("mv1", [P, CH, TPC, 2])
        sum1 = sb("sum1", [P, CH, TPC])
        neg_mean1 = sb("neg_mean1", [P, CH, TPC])
        sq_sum1 = sb("sq_sum1", [P, CH, TPC])
        ve1 = sb("ve1", [P, CH, TPC])
        rs1 = sb("rs1", [P, CH, TPC])
        bn2 = sb("bn2", [P, CH, TPC, 6])
        mv2 = sb("mv2", [P, CH, TPC, 2])
        ve2 = sb("ve2", [P, CH, TPC])
        rs2 = sb("rs2", [P, CH, TPC])
        mhalf = sb("mhalf", [P, TPC])
        x1 = sb("x1", [P, TILES, C])
        xf = sb("xf", [P, TILES, C])
        mn = sb("mn", [P, CH, TPC])
        sm = sb("sm", [P, CH, TPC])
        rsm = sb("rsm", [P, CH, TPC])
        S = sb("S", [P, TILES, E])
        key = sb("key", [P, CH, P])
        junk = sb("junk", [P, DVE_KEYS], f16)
        junk_a = sb("junk_a", [P, CH * P], f16)
        cnt_a = sb("cnt_a", [P, 1], f16)
        keys2 = key[:, :, :].rearrange("p g n -> p (g n)")
        cand = sb("cand", [P, 1])
        above = sb("above", [P, 1])
        low = sb("low", [P, 1])
        high = sb("high", [P, 1])
        top8 = sb("top8", [P, 8])
        top8t = sb("top8t", [8, P])
        missed = sb("missed", [P, 4], f16)
        cands = sb("cands", [E, 2, CANDS])
        falling = sb("falling", [E, CANDS])
        picked = sb("picked", [E, CANDS])
        place = sb("place", [E, 1])
        reached = sb("reached", [E, CANDS])
        n_reached = sb("n_reached", [E, 1])
        thr32 = sb("thr32", [E, 1])
        thr_row = sb("thr_row", [1, P])
        flag = sb("flag", [1, 1], i32)
        over = sb("over", [P, 1])
        under = sb("under", [P, 1])
        binade = sb("binade", [P, 1])
        step = sb("step", [P, 1])
        hit = sb("hit", [P, 1])
        cnt = sb("cnt", [P, 1], f16)
        gt = sb("gt", [P, CH * P], f16)
        eq = sb("eq", [P, CH * P], f16)
        rank = sb("rank", [P, CH * P], f16)
        tie_tot = sb("tie_tot", [P, 1], f16)
        lim = sb("lim", [P, 1])
        tie_ok = sb("tie_ok", [P, CH * P], f16)
        sel = sb("sel", [P, CH * P], f16)
        selT = sb("selT", [P, E, TILES], f16)
        selT_v = selT[:, :, :].rearrange("p e (u g) -> p g u e", u=TPC)
        tot = sb("tot", [P, GROUPS], f16)
        base = sb("base", [P, GROUPS])
        bend = sb("bend", [P, GROUPS])
        cum = sb("cum", [P, GROUPS, P + 2], f16)
        after = sb("after", [P, GROUPS, P], f16)
        onehot = sb("onehot", [P, GROUPS, P], f16)
        junk2 = sb("junk2", [P, P], f16)
        below = sb("below", [P, E])
        idx = sb("idx", [P, E], i32)
        wup = sb("wup", [P, GROUPS, DFF])
        bup = sb("bup", [P, 3, GROUPS])
        wdn = sb("wdn", [P, E, 2, C])
        wdn2 = sb("wdn2", [FR + 1, E, C])
        xg = sb("xg", [P, E, ROW])
        xgT = sb("xgT", [P, 2, 512])
        act = sb("act", [P, 2, 3, 512])
        eo = X[:, :, :].rearrange("p g (q c) -> p (g q) c", c=C)
        zero = sb("zero", [P, 1024])
        upto = xg[:, :, :].rearrange("p e c -> p (e c)")[:, TOK:TOK + CH * P]
        xT = xg[:, :, :].rearrange("p e c -> p (e c)")[:, 0:TOK].rearrange("p (g u c) -> p g u c", g=CH, u=TPC)
        lg = act[:, 0, :, :].rearrange("p j n -> p (j n)")[:, 0:CH * P].rearrange("p (g u e) -> p g u e", g=CH, u=TPC)
        pr = act[:, 1, :, :].rearrange("p j n -> p (j n)")[:, 0:CH * P].rearrange("p (g u e) -> p g u e", g=CH, u=TPC)
        y0, y1, ysum, yo = x1, xf, x1, X

        PZ = pb("PZ", [P, 4, 512])
        PT = pb("PT", [P, 2, 512])
        PM = pb("PM", [P, 2, 512])

        s_const = sem("constants_loaded")
        s_const16 = sem("counting_constants_loaded")
        s_v = sem("v_loaded")
        s_router = sem("router_loaded")
        s_x = [sem(f"x_loaded{g}") for g in range(CH)]
        s_wup = sem("w_up_loaded")
        s_wdn = sem("w_down_loaded")
        s_bup = sem("b_up_loaded")
        s_zero = sem("zero_ready")
        s_set = sem("w_setup_pe")
        s_setv = sem("w_setup_dve")
        s_vc = sem("v_products_ready")
        s_seta = sem("w_setup_act")
        s_fill = sem("fills_ready")
        s_wst = sem("stage_w_ready")
        s_wones = sem("warm_one_ready")
        s_top8 = sem("top8_ready")
        s_top8t = sem("top8_transposed")
        s_top8ts = sem("top8_transposed_in_sbuf")
        s_cands = sem("candidates_by_expert")
        s_high = sem("bracket_ready")
        s_fsel = sem("full_selection_ready")
        s_missed = sem("checks_ready")
        s_nmissed = sem("checks_summed")
        s_thr = sem("threshold_ready")
        s_thrt = sem("threshold_transposed")
        s_thrrow = sem("threshold_row_ready")
        s_thrcol = sem("threshold_column_ready")
        s_flag = sem("flag_ready")
        s_full = sem("full_search_chain")
        s_fcnt = sem("full_counts_ready")
        s_fsum = sem("full_count_sums_ready")
        s_vsq = sem("v_square_sums_ready")
        s_cand = sem("candidate_ready")
        s_cnta = sem("sign_sums_ready")
        s_bias = sem("logits_biased")
        s_smr = sem("softmax_scale_ready")
        s_selp2 = sem("selection_copied_by_act")
        s_cuma = sem("prefix_counts_of_act_ready")
        dch = sem("dve_chain")
        ach = sem("act_chain")
        pch = sem("pool_chain")
        s_xt = sem("x_transposed")
        s_xts = sem("x_transposed_in_sbuf")
        s_z = sem("mixed_ready")
        s_st1 = sem("channel_stats_ready")
        s_rs1 = sem("channel_rstd_ready")
        s_x1 = sem("residual_ready")
        s_st2 = sem("token_stats_ready")
        s_sta = sem("channel_square_sums_ready")
        s_xf = sem("normalised_ready")
        s_zfree = sem("mixed_used")
        s_lg = sem("logits_ready")
        s_exp = sem("exp_ready")
        s_S = sem("softmax_ready")
        s_sT = sem("softmax_transposed")
        s_key = sem("keys_ready")
        s_rows_x = sem("rows_x_stored")
        s_rows_s = sem("rows_s_stored")
        s_acc0 = sem("acc0_filled")
        s_acc1 = sem("acc1_filled")
        s_cnt = sem("counts_ready")
        s_sum = sem("count_sums_ready")
        s_tie = sem("tie_totals_ready")
        s_tieb = sem("tie_bases_ready")
        s_sel = sem("selection_ready")
        s_selp = sem("selection_transposed")
        s_selT = sem("selection_transposed_in_sbuf")
        s_cum = sem("prefix_counts_ready")
        s_tot = sem("tile_totals_ready")
        s_base = sem("tile_bases_ready")
        s_oh = sem("onehot_ready")
        s_find = sem("slot_rows_ready")
        s_idx = sem("indices_ready")
        s_g = [sem(f"gathered{k}") for k in range(len(UNITS))]
        s_gT = sem("gathered_transposed")
        s_gTs = sem("gathered_transposed_in_sbuf")
        s_up = sem("up_ready")
        s_act = sem("activated")
        s_dn = sem("down_ready")
        s_eo = sem("expert_out_ready")
        s_sc = [sem(f"scattered{i}") for i in range(2)]
        s_y = [sem(f"y_loaded{g}") for g in range(CH)]
        s_ys = sem("y_summed")
        s_yT = sem("y_transposed")
        s_yo = sem("y_out_ready")
        s_out = sem("out_stored")

        block = ctx.enter_context(nc.Block())

        x_v = x.rearrange("(u k) c (h n) -> k h c u n", k=PIX // 64, h=2)
        out_v = out.rearrange("(u k) c (h n) -> k h c u n", k=PIX // 64, h=2)
        rows_v = rows.rearrange("(u g p) c -> g p u c", u=TPC, p=P)
        acc_v = [a.rearrange("(u g p) c -> g p u c", u=TPC, p=P) for a in acc]

        def down_bank(e):
            return (PZ[:, 2, 0:C], PZ[:, 3, 0:C], PM[:, 1, 0:C])[e % 3]

        def b4(t):
            return t.unsqueeze(2).to_broadcast([P, TPC, E])

        def per_chunk(t, g):
            return t[:, g * TPC:(g + 1) * TPC, :]

        @block.sync
        def _(sp):
            sp.dma_start(v_raw[:, :], V).then_inc(s_v, 16)
            sp.dma_start(k32[:, :], c32).then_inc(s_const, 16)
            for g in range(CH):
                sp.dma_start(X[:, g, :].rearrange("p (u n) -> p u n", u=TPC), x_v[g // 2, g % 2]).then_inc(s_x[g], 16)
            sp.dma_start(k16[:, :], c16).then_inc(s_const16, 16)
            sp.dma_start(kh16[:, :], ch16).then_inc(s_const16, 16)
            sp.dma_start(wup[:, :, :], w_up.rearrange("g c f -> c g f")).then_inc(s_wup, 16)
            for j, (f0, fn) in enumerate(FF):
                sp.dma_start(bup[0:fn, j, :], b_up[f0:f0 + fn, :]).then_inc(s_bup, 16)
            for j in range(2):
                sp.dma_start(wdn[:, :, j, :], w_down[:, j * P:(j + 1) * P, :].rearrange("e f c -> f e c")).then_inc(s_wdn, 16)
            sp.dma_start(wdn2[0:FR, :, :], w_down[:, 2 * P:DFF, :].rearrange("e f c -> f e c")).then_inc(s_wdn, 16)
            sp.dma_start(wdn2[FR:FR + 1, :, :], b_down.rearrange("(o e) c -> o e c", o=1)).then_inc(s_wdn, 16)
            sp.wait_ge(s_zero, 1)
            for q in range(4):
                sp.dma_start(acc[1][q * 1024:(q + 1) * 1024, :].rearrange("(p k) c -> p (k c)", p=P), zero[:, :]).then_inc(s_acc1, 16)
            for g in range(CH + 2):
                if g < CH:
                    sp.wait_ge(s_x1, TPC * (g + 1))
                    sp.dma_start(acc_v[0][g], per_chunk(x1, g)).then_inc(s_acc0, 16)
                if g >= 2:
                    sp.wait_ge(s_S, g - 1)
                    sp.dma_start(rows_v[g - 2, :, :, C:ROW], per_chunk(S, g - 2)).then_inc(s_rows_s, 16)
            for g in range(CH):
                sp.wait_ge(s_xf, g + 1)
                sp.dma_start(rows_v[g, :, :, 0:C], per_chunk(xf, g)).then_inc(s_rows_x, 16)
            sp.wait_ge(s_rows_x, 16 * CH)
            sp.wait_ge(s_sc[1], 16 * INTO.count(1))
            for g in range(CH):
                sp.dma_start(per_chunk(y1, g), acc_v[1][g]).then_inc(s_y[g], 16)
            sp.wait_ge(s_sc[0], 16 * INTO.count(0))
            for g in range(CH):
                sp.dma_start(per_chunk(y0, g), acc_v[0][g]).then_inc(s_y[g], 16)
            for g in range(CH):
                sp.wait_ge(s_yo, g + 1)
                sp.dma_start(out_v[g // 2, g % 2], yo[:, g, :].rearrange("p (u n) -> p u n", u=TPC)).then_inc(s_out, 16)
            sp.wait_ge(s_out, 16 * CH)

        @block.gpsimd
        def _(pool):
            nch = [0]

            def link(ins):
                nch[0] += 1
                ins.then_inc(pch, 1)
                pool.wait_ge(pch, nch[0])

            link(nc.gpsimd.memset(mhalf[:, :], -0.5))
            nc.gpsimd.memset(zero[:, :], 0.0).then_inc(s_zero, 1)

            def channel_rstd(g):
                if g in ACT_STATS:
                    pool.wait_ge(s_sta, ACT_STATS.index(g) + 1)
                    link(nc.gpsimd.tensor_scalar(ve1[:, g, :], sq_sum1[:, g, :], 1.0 / C, 1e-6, ALU.mult, ALU.add))
                else:
                    pool.wait_ge(s_st1, TPC * (DVE_STATS.index(g) + 1))
                    link(nc.gpsimd.tensor_scalar(ve1[:, g, :], mv1[:, g, :, 1], 1e-6, None, ALU.add))
                nc.gpsimd.tensor_tensor(rs1[:, g, :], ve1[:, g, :], mhalf[:, :], ALU.pow).then_inc(s_rs1, 1)

            for g in range(XAHEAD):
                channel_rstd(g)
            for g in range(CH + SCALE_LAG):
                if g < CH:
                    pool.wait_ge(s_st2, g + 1)
                    link(nc.gpsimd.tensor_tensor(rs2[:, g, :], ve2[:, g, :], mhalf[:, :], ALU.pow))
                    pool.wait_ge(s_zfree, g + 1)
                    L = lg[:, g, :, :]
                    link(nc.gpsimd.tensor_tensor(L, L, b4(rs2[:, g, :]), ALU.mult))
                    if g == 0:
                        pool.wait_ge(s_router, 32)
                    nc.gpsimd.tensor_tensor(L, L, router_b[:, :].unsqueeze(1).to_broadcast([P, TPC, E]), ALU.subtract).then_inc(s_bias, 1)
                if 2 <= g < 2 + CH - XAHEAD:
                    channel_rstd(XAHEAD - 2 + g)
                if g >= SCALE_LAG:
                    h = g - SCALE_LAG
                    pool.wait_ge(s_smr, h + 1)
                    nc.gpsimd.tensor_tensor(per_chunk(S, h), pr[:, h, :, :], b4(rsm[:, h, :]), ALU.mult).then_inc(s_S, 1)
            for g in range(CH):
                mean2 = mv2[:, g, :, 0].unsqueeze(2).to_broadcast([P, TPC, C])
                link(nc.gpsimd.tensor_tensor(per_chunk(xf, g), per_chunk(x1, g), mean2, ALU.subtract))
                nc.gpsimd.tensor_tensor(per_chunk(xf, g), per_chunk(xf, g), rs2[:, g, :].unsqueeze(2).to_broadcast([P, TPC, C]),
                                        ALU.mult).then_inc(s_xf, 1)
            pool.wait_ge(s_S, CH)
            pool.wait_ge(s_xf, CH)
            nc.gpsimd.memset(act[64:P, :, 2, :], 1.0).then_inc(s_fill, 1)

            def gather(e):
                pool.wait_ge(s_idx, e + 1)
                nc.gpsimd.indirect_dma_start(
                    out=xg[:, e, :], out_offset=None, in_=rows[:, :],
                    in_offset=bass.IndirectOffsetOnAxis(ap=idx[:, e:e + 1], axis=0)).then_inc(s_g[UNIT_OF[e]], 16)

            def scatter(e):
                pool.wait_ge(s_eo, e + 1)
                i = INTO[e]
                if e >= 2:
                    pool.wait_ge(s_sc[i], 16 * INTO[:e].count(i))
                nc.gpsimd.indirect_dma_start(
                    out=acc[i][:, :], out_offset=bass.IndirectOffsetOnAxis(ap=idx[:, e:e + 1], axis=0),
                    in_=eo[:, e, :], in_offset=None, compute_op=ALU.add).then_inc(s_sc[i], 16)

            pool.wait_ge(s_rows_x, 16 * CH)
            pool.wait_ge(s_rows_s, 16 * CH)
            pool.wait_ge(s_acc0, 16 * CH)
            pool.wait_ge(s_acc1, 16 * 4)
            gathered = 0
            for e in range(E):
                while gathered < min(E, LEAD + int(CLOSING * e)):
                    gather(gathered)
                    gathered += 1
                scatter(e)

        @block.scalar
        def _(a):
            nch = [0]

            def link(ins):
                nch[0] += 1
                ins.then_inc(ach, 1)
                a.wait_ge(ach, nch[0])

            a.dma_start(router[:, :], w_router).then_inc(s_router, 16)
            a.dma_start(router_b[:, :], b_router.rearrange("(o e) -> o e", o=1).to_broadcast([P, E])).then_inc(s_router, 16)
            a.wait_ge(s_wones, 1)
            nc.scalar.activation(warm[:, 1:2], warm[:, 0:1], ACT.Sqrt)
            a.wait_ge(s_vsq, 1)
            nc.scalar.activation(v_norm[:, 1:2], v_norm[:, 0:1], ACT.Sqrt).then_inc(s_seta, 1)

            def copy_x(g):
                a.wait_ge(s_xt, g + 1)
                if g in ACT_STATS:
                    for u in range(TPC):
                        ins = nc.scalar.activation(xT[:, g, u, :], PT[:, g % 2, u * P:(u + 1) * P], ACT.Copy,
                                                   accum_out=sum1[:, g, u:u + 1])
                    ins.then_inc(s_xts, 1)
                    a.wait_ge(s_xts, g + 1)
                    link(nc.scalar.activation(neg_mean1[:, g, :], sum1[:, g, :], ACT.Copy, scale=-1.0 / C))
                    for u in range(TPC):
                        ins = nc.scalar.activation(xf[:, g * TPC + u, :], xT[:, g, u, :], ACT.Square, bias=neg_mean1[:, g, u:u + 1],
                                                   accum_out=sq_sum1[:, g, u:u + 1])
                    ins.then_inc(s_sta, 1)
                else:
                    nc.scalar.activation(xT[:, g, :, :], PT[:, g % 2, :].rearrange("p (u c) -> p u c", u=TPC), ACT.Copy).then_inc(s_xts, 1)

            def exps(g):
                a.wait_ge(s_lg, g + 1)
                for u in range(TPC):
                    ins = nc.scalar.activation(pr[:, g, u, :], lg[:, g, u, :], ACT.Exp, bias=mn[:, g, u:u + 1], scale=-1.0,
                                               accum_out=sm[:, g, u:u + 1])
                ins.then_inc(s_exp, 1)

            for g in range(XAHEAD):
                copy_x(g)

            def keys(g):
                a.wait_ge(s_sT, g + 1)
                nc.scalar.activation(key[:, g, :], PM[:, g % 2, 0:P], ACT.Copy, bias=FLOOR).then_inc(s_key, 1)

            done = 0
            for g in range(CH + 1):
                if g + XAHEAD < CH:
                    copy_x(g + XAHEAD)
                if g == CH:
                    while done < CH - 3:
                        keys(done)
                        done += 1
                if 1 <= g:
                    exps(g - 1)
                if g >= KEYS_LAG:
                    keys(done)
                    done += 1
            while done < CH:
                keys(done)
                done += 1

            a.wait_ge(s_key, CH)
            for j in range(ROUNDS):
                a.wait_ge(s_cand, j + 1)
                with nc.allow_low_precision(reason="a sum of at most ACT_KEYS signs is exact in float16"):
                    nc.scalar.activation(junk_a[:, 0:ACT_KEYS], keys2[:, DVE_KEYS:CH * P], ACT.Sign, bias=cand[:, 0:1], scale=-1.0,
                                         accum_out=cnt_a[:, 0:1]).then_inc(s_cnta, 1)
            a.wait_ge(s_high, 1)
            with nc.allow_low_precision(reason="a sum of at most CH * P signs is exact in float16"):
                nc.scalar.activation(junk_a[:, :], keys2, ACT.Sign, bias=high[:, 0:1], scale=-1.0, accum_out=cnt_a[:, 0:1]).then_inc(s_cnta, 1)
            a.wait_ge(s_selp, 2)
            nc.scalar.activation(selT_v[:, CH // 2:CH, :, :], PT[:, 1, 0:256].bitcast(f16).rearrange("p (g u e) -> p g u e", g=CH // 2, u=TPC),
                                 ACT.Copy).then_inc(s_selp2, 1)
            a.wait_ge(s_base, 2)
            for g in range(GROUPS // 2, GROUPS):
                nc.scalar.activation(cum[:, g, 0:P], PZ[:, 1, (g - GROUPS // 2) * P:(g - GROUPS // 2 + 1) * P], ACT.Identity,
                                     bias=base[:, g:g + 1]).then_inc(s_cuma, 1)
            nc.scalar.activation(warm[:, 1:2], warm[:, 0:1], ACT.Silu)
            for k, (e0, n) in enumerate(UNITS):
                a.wait_ge(s_gT, k + 1)
                if k >= 2:
                    a.wait_ge(s_up, 3 * (k - 1))
                nc.scalar.activation(xgT[:, k % 2, 0:n * P], PT[:, 0, 0:n * P], ACT.Copy).then_inc(s_gTs, 1)
                if k == 0:
                    a.wait_ge(s_bup, 48)
                    a.wait_ge(s_fill, 1)
                for j, (f0, fn) in enumerate(FF):
                    a.wait_ge(s_up, 3 * k + j + 1)
                    if k >= 2 and j == 0:
                        a.wait_ge(s_dn, UNITS[k - 1][0])
                    src = PT[0:fn, 1, 0:n * P] if (3 * k + j) % 2 == 0 else PM[0:fn, 0, 0:n * P]
                    nc.scalar.activation(act[0:fn, k % 2, j, 0:n * P], src, ACT.Silu, bias=bup[0:fn, j, e0 // PER:e0 // PER + 1]).then_inc(s_act, 1)
            for g in range(CH):
                a.wait_ge(s_yT, g + 1)
                nc.scalar.activation(yo[:, g, :], PT[:, g % 2, :], ACT.Copy).then_inc(s_yo, 1)

        @block.vector
        def _(v):
            nch = [0]

            def link(ins):
                nch[0] += 1
                ins.then_inc(dch, 1)
                v.wait_ge(dch, nch[0])

            tiles, waiting = [0], []

            def join_stats1():
                if waiting:
                    g, u, at = waiting.pop()
                    v.wait_ge(dch, at)
                    nc.vector.bn_aggr(mv1[:, g, u, :], bn1[:, g, u, :]).then_inc(s_st1, 1)

            def stats1(n=1):
                for _ in range(n):
                    join_stats1()
                    g, u = DVE_STATS[tiles[0] // TPC], tiles[0] % TPC
                    if u == 0:
                        v.wait_ge(s_xts, g + 1)
                    nc.vector.bn_stats(bn1[:, g, u, :], xT[:, g, u, :]).then_inc(dch, 1)
                    nch[0] += 1
                    waiting.append((g, u, nch[0]))
                    tiles[0] += 1

            nc.vector.memset(warm[:, 0:1], 1.0).then_inc(s_wones, 1)
            v.wait_ge(s_v, 16)
            nc.vector.scalar_tensor_tensor(v_sq[:, :], v_raw[:, :], 1.0, v_raw[:, :], ALU.mult, ALU.mult, accum_out=v_norm[:, 0:1]).then_inc(s_vsq, 1)
            v.wait_ge(s_const, 16)
            nc.vector.tensor_copy(cb[:, 0:C], centre)
            v.wait_ge(s_set, 1)
            nc.vector.tensor_scalar(cb[:, C:C + E], PM[:, 1, 0:E], -1.0, None, ALU.mult)
            nc.vector.tensor_scalar(stage_w[:, C + E:C + 2 * E], PM[:, 1, 0:E], -1.0, None, ALU.mult).then_inc(s_setv, 1)
            v.wait_ge(s_seta, 1)
            link(nc.vector.tensor_scalar(v_norm[:, 1:2], v_norm[:, 1:2], 1e-8, None, ALU.add))
            link(nc.vector.reciprocal(v_norm[:, 2:3], v_norm[:, 1:2]))
            nc.vector.tensor_scalar(v_vb[:, 0:C], v_raw[:, :], v_norm[:, 2:3], None, ALU.mult).then_inc(s_setv, 1)
            v.wait_ge(s_set, 2)
            nc.vector.tensor_copy(v_t[:, :], PM[:, 0, 0:HH]).then_inc(s_setv, 1)
            v.wait_ge(s_set, 3)
            nc.vector.tensor_tensor(gm[:, :, :], PM[0:HH, 1, 0:HH].unsqueeze(1).to_broadcast([HH, LEVELS, HH]),
                                    c_("merge", HH).rearrange("p (l h) -> p l h", l=LEVELS), ALU.mult)
            link(nc.vector.tensor_tensor(g0[:, :], PM[0:HH, 1, 0:HH], c_("merge0", HH), ALU.mult))
            nc.vector.scalar_tensor_tensor(Tt[:, :], gm[:, 0, :], -4.0, c_("two_eye", HH), ALU.mult, ALU.add)
            nc.vector.scalar_tensor_tensor(Tm[:, :], g0[:, :], -4.0, c_("two_eye", HH), ALU.mult, ALU.add).then_inc(s_setv, 1)
            v.wait_ge(s_set, 4)
            nc.vector.tensor_copy(v_c[:, :], PZ[0:HH, 0, 0:C])
            nc.vector.tensor_copy(v_vb[:, C:C + E], PZ[0:HH, 0, C:C + E]).then_inc(s_vc, 1)
            for l in range(1, LEVELS):
                if l > 2:
                    stats1()
                v.wait_ge(s_set, 3 + 2 * l)
                nc.vector.tensor_copy(Am[:, :], PM[0:HH, 0, 0:HH]).then_inc(s_setv, 1)
                if l > 1:
                    stats1()
                v.wait_ge(s_set, 4 + 2 * l)
                nc.vector.tensor_tensor(Tm[:, :], Tm[:, :], PM[0:HH, 1, 0:HH], ALU.subtract)
                nc.vector.tensor_tensor(Tt[:, :], Tt[:, :], PM[0:HH, 1, HH:2 * HH], ALU.subtract).then_inc(s_setv, 1)
            n = 2 + 2 * LEVELS
            stats1(1)
            v.wait_ge(s_set, n + 1)
            nc.vector.tensor_copy(t_vb[:, :], PM[0:HH, 0, 0:C + E]).then_inc(s_setv, 1)
            stats1(2)
            join_stats1()
            v.wait_ge(s_set, n + 2)
            nc.vector.tensor_tensor(stage_w[:, 0:C + E], cb[:, :], PM[:, 1, 0:C + E], ALU.subtract).then_inc(s_wst, 1)

            def zview(g, lo, n):
                return PZ[:, 2 * (g % 2):2 * (g % 2) + 2, 0:2 * (C + 2 * E)].rearrange("p k (w c) -> p k w c", w=2)[:, :, :, lo:lo + n]

            def residual(g):
                v.wait_ge(s_rs1, g + 1)
                for u in range(TPC):
                    if u % 2 == 0:
                        v.wait_ge(s_z, 2 * g + u // 2 + 1)
                    z = PZ[:, 2 * (g % 2) + u // 2, (u % 2) * (C + 2 * E):(u % 2) * (C + 2 * E) + C]
                    nc.vector.scalar_tensor_tensor(x1[:, g * TPC + u, :], z, rs1[:, g, u:u + 1], xT[:, g, u, :],
                                                   ALU.mult, ALU.add).then_inc(s_x1, 1)

            def stats2(g):
                v.wait_ge(s_x1, TPC * (g + 1))
                for u in range(TPC):
                    ins = nc.vector.bn_stats(bn2[:, g, u, :], x1[:, g * TPC + u, :])
                nch[0] += 1
                ins.then_inc(dch, 1)
                return nch[0]

            def aggregate(g, at):
                v.wait_ge(dch, at)
                for u in range(TPC):
                    ins = nc.vector.bn_aggr(mv2[:, g, u, :], bn2[:, g, u, :])
                nch[0] += 1
                ins.then_inc(dch, 1)
                return nch[0]

            def for_rstd(g, at):
                v.wait_ge(dch, at)
                nc.vector.tensor_scalar(ve2[:, g, :], mv2[:, g, :, 1], 1e-5, None, ALU.add).then_inc(s_st2, 1)

            def b22(t):
                return t.rearrange("p (k w) -> p k w", k=2).unsqueeze(3).to_broadcast([P, 2, 2, E])

            def logits(g):
                L22 = lg[:, g, :, :].rearrange("p (k w) e -> p k w e", k=2)
                nc.vector.tensor_tensor(L22, zview(g, C, E), b22(rs1[:, g, :]), ALU.mult).then_inc(dch, 1)
                nch[0] += 1
                return nch[0]

            def logits_sum(g, at):
                L22 = lg[:, g, :, :].rearrange("p (k w) e -> p k w e", k=2)
                v.wait_ge(dch, at)
                nc.vector.tensor_tensor(L22, L22, zview(g, C + E, E), ALU.add).then_inc(s_zfree, 1)

            def largest(g):
                v.wait_ge(s_bias, g + 1)
                nc.vector.tensor_reduce(mn[:, g, :], lg[:, g, :, :], AX.X, ALU.min).then_inc(s_lg, 1)

            def softmax_scale(g):
                v.wait_ge(s_exp, g + 1)
                nc.vector.reciprocal(rsm[:, g, :], sm[:, g, :]).then_inc(s_smr, 1)

            for g in range(CH + SCALE_LAG):
                more = LATE_STATS <= g < LATE_STATS + len(DVE_STATS) - 2
                if g < CH:
                    residual(g)
                    product = logits(g)
                    stats = stats2(g)
                    logits_sum(g, product)
                    stats = aggregate(g, stats)
                if 1 <= g <= CH:
                    largest(g - 1)
                if g < CH:
                    for_rstd(g, stats)
                if more:
                    stats1(TPC)
                join_stats1()
                if g >= SCALE_LAG:
                    softmax_scale(g - SCALE_LAG)

            v.wait_ge(s_key, CH)

            def pick(out, j, lower, upper):
                return nc.vector.scalar_tensor_tensor(out[:, :], PM[:, j % 2, 0:1], lower[:, 0:1], upper[:, :], ALU.max, ALU.min)

            def scaled(out, a):
                return nc.vector.tensor_scalar(out[:, :], cand[:, :], a, None, ALU.mult)

            def moved(out, a):
                return nc.vector.scalar_tensor_tensor(out[:, :], binade[:, :], a, cand[:, :], ALU.mult, ALU.add)

            nc.vector.memset(cand[:, :], 2.0 ** (LOW_EXP + 2 ** (EXP_ROUNDS - 1))).then_inc(s_cand, 1)
            for j in range(ROUNDS):
                v.wait_ge(s_cand, j + 1)
                nc.vector.tensor_scalar(junk[:, :], keys2[:, 0:DVE_KEYS], cand[:, 0:1], None, ALU.is_ge, ALU.add, accum_out=cnt[:, 0:1]).then_inc(s_cnt, 1)
                if j < EXP_ROUNDS - 1:
                    f = 2.0 ** (2 ** (EXP_ROUNDS - 2 - j))
                    scaled(over, f)
                    link(scaled(under, 1.0 / f))
                    v.wait_ge(s_sum, j + 1)
                    pick(cand, j, under, over).then_inc(s_cand, 1)
                elif j == EXP_ROUNDS - 1:
                    scaled(step, 0.5)
                    scaled(over, 1.5)
                    nc.vector.tensor_copy(binade[:, :], cand[:, :])
                    link(scaled(under, 0.75))
                    v.wait_ge(s_sum, j + 1)
                    pick(cand, j, under, over).then_inc(s_cand, 1)
                    link(pick(binade, j, step, binade))
                else:
                    size = 2.0 ** (EXP_ROUNDS - 1 - j)
                    if j < ROUNDS - 1:
                        moved(over, size / 2)
                        link(moved(under, -size / 2))
                        v.wait_ge(s_sum, j + 1)
                        pick(cand, j, under, over).then_inc(s_cand, 1)
                    else:
                        moved(over, size)
                        link(moved(under, -size))
                        v.wait_ge(s_sum, j + 1)
                        pick(high, j, cand, over).then_inc(s_high, 1)
                        link(pick(low, j, under, cand))
                        v.wait_ge(s_high, 1)

            link(nc.vector.scalar_tensor_tensor(upto[:, :], keys2, high[:, 0:1], keys2, ALU.is_le, ALU.mult))
            nc.vector.max(top8[:, :], upto[:, :]).then_inc(s_top8, 1)
            v.wait_ge(s_top8, 1)
            nc.vector.tensor_scalar(missed[:, 0:1], top8[:, 7:8], low[:, 0:1], None, ALU.is_ge).then_inc(s_missed, 1)
            v.wait_ge(s_top8t, 1)
            nc.vector.tensor_copy(top8t[:, :], PT[0:8, 0, 0:P]).then_inc(s_top8ts, 1)
            v.wait_ge(s_cands, 1)
            link(nc.vector.tensor_copy(cands[:, 0, :], PT[0:E, 1, 0:CANDS]))
            for k in range(CANDS // 8):
                link(nc.vector.max(falling[:, 8 * k:8 * k + 8], cands[:, k % 2, :]))
                if k < CANDS // 8 - 1:
                    link(nc.vector.match_replace(cands[:, (k + 1) % 2, :], falling[:, 8 * k:8 * k + 8], cands[:, k % 2, :], -1.0))
            v.wait_ge(s_sum, ROUNDS + 1)
            link(nc.vector.tensor_scalar(place[:, :], PM[0:E, ROUNDS % 2, 0:1], -0.25, float(K - 1 - TOK // 2), ALU.mult, ALU.add))
            nc.vector.scalar_tensor_tensor(picked[:, :], slots16[0:E, 0:CANDS], place[:, 0:1], falling[:, :], ALU.is_equal, ALU.mult,
                                           accum_out=thr32[:, 0:1]).then_inc(s_thr, 1)
            nc.vector.tensor_scalar(missed[0:E, 1:2], falling[:, 0:1], high[0:E, 0:1], None, ALU.is_ge)
            v.wait_ge(s_thr, 1)
            link(nc.vector.tensor_scalar(reached[:, :], falling[:, :], thr32[:, 0:1], None, ALU.is_ge, ALU.add, accum_out=n_reached[:, 0:1]))
            nc.vector.scalar_tensor_tensor(missed[0:E, 3:4], place[:, :], 1.0, n_reached[:, :], ALU.add, ALU.not_equal)
            nc.vector.tensor_scalar(missed[0:E, 2:3], thr32[:, 0:1], low[0:E, 0:1], None, ALU.is_lt).then_inc(s_missed, 1)
            v.wait_ge(s_thrt, 1)
            nc.vector.tensor_copy(thr_row[:, :].rearrange("p (u e) -> p u e", u=QUARTERS),
                                  PT[0:1, 0, 0:E].unsqueeze(1).to_broadcast([1, QUARTERS, E])).then_inc(s_thrrow, 1)
            v.wait_ge(s_nmissed, 1)
            nc.vector.tensor_copy(flag[:, :], PM[0:1, 1, 0:1]).then_inc(s_flag, 1)
            v.wait_ge(s_thrcol, 1)
            link(nc.vector.tensor_copy(cand[:, :], PT[:, 1, 0:1]))
            for h in range(2):
                o = slice(h * CH * P // 2, (h + 1) * CH * P // 2)
                nc.vector.tensor_scalar(sel[:, o], keys2[:, o], cand[:, 0:1], None, ALU.is_ge).then_inc(s_sel, 1)
            v.wait_ge(s_flag, 1)
            failed = v.alloc_register("failed_v")
            v.reg_load(failed, flag[0:1, 0:1])

            with v.If_ne(failed, 0):
                v.wait_ge(s_sel, 2)
                nfull = [0]

                def full_link(ins, i=0, each=0):
                    nfull[0] += 1
                    ins.then_inc(s_full, 1)
                    v.wait_ge(s_full, i * each + nfull[0])

                def full_count(n):
                    nc.vector.tensor_scalar(gt[:, :], keys2, above[:, 0:1], None, ALU.is_ge, ALU.add, accum_out=cnt[:, 0:1]).then_inc(s_fcnt, 1)
                    v.wait_ge(s_fsum, n)

                full_link(nc.vector.memset(cand[:, :], FLOOR))
                for j in range(FULL_EXP_ROUNDS):
                    f = 2.0 ** (2 ** (FULL_EXP_ROUNDS - 1 - j))
                    full_link(nc.vector.tensor_scalar(above[:, :], cand[:, :], f, None, ALU.mult))
                    full_count(j + 1)
                    full_link(nc.vector.tensor_scalar(hit[:, :], PM[:, 0, 0:1], float(K), float(np.float32(f - 1.0)), ALU.is_ge, ALU.mult))
                    full_link(nc.vector.scalar_tensor_tensor(cand[:, :], hit[:, :], 1.0, cand[:, :], ALU.add, ALU.mult))
                full_link(nc.vector.tensor_copy(step[:, :], cand[:, :]))
                with v.Fori(0, FULL_MAN_ROUNDS) as i:
                    full_link(nc.vector.tensor_scalar(step[:, :], step[:, :], 0.5, None, ALU.mult), i, 4)
                    full_link(nc.vector.tensor_tensor(above[:, :], cand[:, :], step[:, :], ALU.add), i, 4)
                    full_count(i + FULL_EXP_ROUNDS + 1)
                    full_link(nc.vector.tensor_scalar(hit[:, :], PM[:, 0, 0:1], float(K), None, ALU.is_ge), i, 4)
                    full_link(nc.vector.scalar_tensor_tensor(cand[:, :], hit[:, :], step[:, 0:1], cand[:, :], ALU.mult, ALU.add), i, 4)
                nfull[0] += 4 * (FULL_MAN_ROUNDS - 1)

                full_link(nc.vector.tensor_scalar(eq[:, :], keys2, cand[:, 0:1], None, ALU.is_equal))
                full_link(nc.vector.tensor_tensor_scan(rank[:, :], eq[:, :], eq[:, :], 0.0, ALU.add, ALU.max))
                nc.vector.tensor_copy(tie_tot[:, :], rank[:, CH * P - 1:CH * P]).then_inc(s_tie, 1)
                nc.vector.tensor_scalar(gt[:, :], keys2, cand[:, 0:1], None, ALU.is_gt, ALU.add, accum_out=cnt[:, 0:1]).then_inc(s_fcnt, 1)
                v.wait_ge(s_tieb, 1)
                full_link(nc.vector.tensor_scalar(lim[:, :], PM[:, 1, 0:1], -1.0, float(K), ALU.mult, ALU.add))
                full_link(nc.vector.scalar_tensor_tensor(tie_ok[:, :], rank[:, :], lim[:, 0:1], eq[:, :], ALU.is_le, ALU.mult))
                nc.vector.tensor_tensor(sel[:, :], gt[:, :], tie_ok[:, :], ALU.add).then_inc(s_fsel, 1)

            v.wait_ge(s_selp, 1)
            nc.vector.tensor_copy(selT_v[:, 0:CH // 2, :, :], PT[:, 0, 0:256].bitcast(f16).rearrange("p (g u e) -> p g u e", g=CH // 2, u=TPC)).then_inc(s_selT, 1)

            v.wait_ge(s_cum, 1)
            link(nc.vector.tensor_copy(tot[:, :], PZ[:, 0:2, :].rearrange("p k (g n) -> p (k g) n", n=P)[:, :, P - 1]))
            nc.vector.tensor_copy(cum[:, :, P:P + 1], c_("tile_start").unsqueeze(1).to_broadcast([P, GROUPS, 1])).then_inc(s_tot, 1)
            v.wait_ge(s_base, 1)
            ins = nc.vector.tensor_copy(base[:, :], PM[:, 1, 0:GROUPS])
            ins.then_inc(s_base, 1)
            v.wait_ge(s_base, 2)
            nc.vector.tensor_tensor(bend[:, :], base[:, :], tot[:, :], ALU.add)
            link(nc.vector.tensor_tensor(cum[:, 0:GROUPS // 2, 0:P], PZ[:, 0, :].rearrange("p (g n) -> p g n", n=P),
                                         base[:, 0:GROUPS // 2].unsqueeze(2).to_broadcast([P, GROUPS // 2, P]), ALU.add))

            def one_hot(g):
                link(nc.vector.tensor_scalar(after[:, g, :], slots16, base[:, g:g + 1], None, ALU.is_ge))
                nc.vector.scalar_tensor_tensor(onehot[:, g, :], slots16, bend[:, g:g + 1], after[:, g, :], ALU.is_lt, ALU.mult).then_inc(s_oh, 1)

            def token_number(e):
                if e >= E:
                    return
                v.wait_ge(s_find, e + 1)
                link(nc.vector.tensor_scalar(junk2[:, :], PZ[:, e % 2, 0:P], c_("slot_col"), None, ALU.is_le, ALU.add,
                                             accum_out=below[:, e:e + 1]))
                nc.vector.tensor_tensor(idx[:, e:e + 1], below[:, e:e + 1], PZ[:, e % 2, P:P + 1], ALU.add).then_inc(s_idx, 1)
                if e % PER == PER - 1 and e // PER + 2 < GROUPS:
                    one_hot(e // PER + 2)

            one_hot(0)
            one_hot(1)
            for e in range(AHEAD):
                token_number(e)
            for e in range(E):
                v.wait_ge(s_dn, e + 1)
                nc.vector.tensor_scalar(eo[:, e, :], down_bank(e), xg[:, e, C + e:C + e + 1], None, ALU.mult).then_inc(s_eo, 1)
                token_number(e + AHEAD)

            for g in range(CH):
                v.wait_ge(s_y[g], 32)
                nc.vector.tensor_tensor(per_chunk(ysum, g), per_chunk(y0, g), per_chunk(y1, g), ALU.add).then_inc(s_ys, 1)

        @block.tensor
        def _(pe):
            mm = nc.tensor.matmul
            tiles = [0]

            def x_transpose(n=1):
                for _ in range(n):
                    g, u = tiles[0] // TPC, tiles[0] % TPC
                    tiles[0] += 1
                    if u == 0:
                        pe.wait_ge(s_x[g], 16)
                        if g >= 2:
                            pe.wait_ge(s_xts, g - 1)
                    ins = nc.tensor.transpose(PT[:, g % 2, u * P:(u + 1) * P], X[:, g, u * P:(u + 1) * P], ident)
                    if u == TPC - 1:
                        ins.then_inc(s_xt, 1)

            pe.wait_ge(s_const, 16)
            pe.wait_ge(s_router, 32)
            v_n = v_vb[:, 0:C]
            mm(PM[:, 1, 0:E], centre, router[:, :], start=True, stop=True).then_inc(s_set, 1)
            pe.wait_ge(s_setv, 2)
            nc.tensor.transpose(PM[:, 0, 0:HH], v_n, c_("ident", HH)[:, 0:HH]).then_inc(s_set, 1)
            x_transpose(1)
            pe.wait_ge(s_setv, 3)
            mm(PM[0:HH, 1, 0:HH], v_t[:, :], v_t[:, :], start=True, stop=True).then_inc(s_set, 1)
            mm(PZ[0:HH, 0, 0:C + E], v_t[:, :], cb[:, :], start=True, stop=True).then_inc(s_set, 1)
            x_transpose(XSLOTS[0])
            for l in range(1, LEVELS):
                pe.wait_ge(s_setv, 2 + 2 * l)
                mm(PM[0:HH, 0, 0:HH], gm[:, l, :], Tm[:, :], start=True, stop=True).then_inc(s_set, 1)
                x_transpose(XSLOTS[2 * l - 1])
                pe.wait_ge(s_setv, 3 + 2 * l)
                mm(PM[0:HH, 1, 0:HH], Tt[:, :], Am[:, :], start=True, stop=True)
                mm(PM[0:HH, 1, HH:2 * HH], Am[:, :], Tt[:, :], start=True, stop=True).then_inc(s_set, 1)
                x_transpose(XSLOTS[2 * l])
            n = 2 + 2 * LEVELS
            pe.wait_ge(s_setv, n)
            pe.wait_ge(s_vc, 1)
            mm(PM[0:HH, 0, 0:C + E], Tt[:, :], v_vb[:, :], start=True, stop=True).then_inc(s_set, 1)
            x_transpose(1)
            pe.wait_ge(s_setv, n + 1)
            mm(PM[:, 1, 0:C + E], v_c[:, :], t_vb[:, :], start=True, stop=True).then_inc(s_set, 1)
            x_transpose(XAHEAD * TPC - tiles[0])

            def keys_transpose(g):
                pe.wait_ge(s_S, g + 1)
                if g >= 2:
                    pe.wait_ge(s_key, g - 1)
                nc.tensor.transpose(PM[:, g % 2, 0:P], per_chunk(S, g).rearrange("p u e -> p (u e)"), ident).then_inc(s_sT, 1)

            pe.wait_ge(s_wst, 1)
            for g in range(CH + KEYS_LAG):
                if g < CH:
                    if g >= 2:
                        pe.wait_ge(s_zfree, g - 1)
                    W_ = C + 2 * E
                    for u in range(TPC):
                        ins = mm(PZ[:, 2 * (g % 2) + u // 2, (u % 2) * W_:(u % 2 + 1) * W_], X[:, g, u * P:(u + 1) * P], stage_w[:, :],
                                 start=True, stop=True)
                        if u % 2:
                            ins.then_inc(s_z, 1)
                if g + XAHEAD < CH:
                    x_transpose(TPC)
                if g >= KEYS_LAG:
                    keys_transpose(g - KEYS_LAG)

            pe.wait_ge(s_key, CH)
            pe.wait_ge(s_const16, 32)
            for j in range(ROUNDS):
                pe.wait_ge(s_cand, j + 1)
                mm(PM[:, j % 2, 0:1], same_expert, sum_bias, start=True, stop=False)
                pe.wait_ge(s_cnt, j + 1)
                mm(PM[:, j % 2, 0:1], same_expert_4, cnt[:, 0:1], start=False, stop=False)
                pe.wait_ge(s_cnta, j + 1)
                mm(PM[:, j % 2, 0:1], same_expert_m2, cnt_a[:, 0:1], start=False, stop=True).then_inc(s_sum, 1)
            pe.wait_ge(s_top8, 1)
            nc.tensor.transpose(PT[0:8, 0, 0:P], top8[:, :], ident).then_inc(s_top8t, 1)
            pe.wait_ge(s_cnta, ROUNDS + 1)
            mm(PM[:, ROUNDS % 2, 0:1], same_expert_m2, cnt_a[:, 0:1], start=True, stop=True).then_inc(s_sum, 1)
            pe.wait_ge(s_top8ts, 1)
            for u in range(QUARTERS):
                ins = nc.tensor.transpose(PT[0:E, 1, 8 * u:8 * u + 8], top8t[:, u * E:(u + 1) * E], ident[0:8, 0:8])
            ins.then_inc(s_cands, 1)
            ones16 = tri16[:, P - 1:P]
            pe.wait_ge(s_thr, 1)
            nc.tensor.transpose(PT[0:1, 0, 0:E], thr32[:, :], ident[0:E, 0:E]).then_inc(s_thrt, 1)
            pe.wait_ge(s_missed, 2)
            mm(PM[0:1, 1, 0:1], missed[:, 0:1], ones16, start=True, stop=False)
            for j in range(1, 4):
                ins = mm(PM[0:1, 1, 0:1], missed[0:E, j:j + 1], ones16[0:E, :], start=False, stop=j == 3)
            ins.then_inc(s_nmissed, 1)
            pe.wait_ge(s_thrrow, 1)
            nc.tensor.transpose(PT[:, 1, 0:1], thr_row[:, :], ident[0:1, 0:1]).then_inc(s_thrcol, 1)
            pe.wait_ge(s_flag, 1)
            failed = pe.alloc_register("failed_pe")
            pe.reg_load(failed, flag[0:1, 0:1])
            with pe.If_ne(failed, 0):
                with pe.Fori(0, FULL_EXP_ROUNDS + FULL_MAN_ROUNDS) as i:
                    pe.wait_ge(s_fcnt, i + 1)
                    mm(PM[:, 0, 0:1], same_expert, cnt[:, 0:1], start=True, stop=True).then_inc(s_fsum, 1)
                pe.wait_ge(s_fcnt, FULL_EXP_ROUNDS + FULL_MAN_ROUNDS + 1)
                mm(PM[:, 1, 0:1], same_expert, cnt[:, 0:1], start=True, stop=False)
                pe.wait_ge(s_tie, 1)
                mm(PM[:, 1, 0:1], earlier_u, tie_tot[:, :], start=False, stop=True).then_inc(s_tieb, 1)
                pe.wait_ge(s_fsel, 1)
            for h in range(2):
                pe.wait_ge(s_sel, h + 1)
                for k in range(CH // 2):
                    g = h * CH // 2 + k
                    ins = nc.tensor.transpose(PT[:, h, 0:256].bitcast(f16)[:, k * P:(k + 1) * P], sel[:, g * P:(g + 1) * P], ident16)
                ins.then_inc(s_selp, 1)
            pe.wait_ge(s_selT, 1)
            pe.wait_ge(s_selp2, 1)
            for g in range(GROUPS):
                ins = mm(PZ[:, g // 4, (g % 4) * P:(g % 4 + 1) * P], selT[:, g * PER:(g + 1) * PER, :].rearrange("p e t -> p (e t)"), tri16,
                         start=True, stop=True)
            ins.then_inc(s_cum, 1)
            pe.wait_ge(s_tot, 1)
            mm(PM[:, 1, 0:GROUPS], earlier_tile, tot[:, :], start=True, stop=True).then_inc(s_base, 1)
            def find(e):
                if e >= E:
                    return
                g, q = e // PER, e % PER
                pe.wait_ge(s_oh, g + 1)
                if e == 0:
                    pe.wait_ge(s_cuma, GROUPS // 2)
                if e >= 2:
                    pe.wait_ge(s_idx, e - 1)
                r = slice(q * TILES, (q + 1) * TILES)
                mm(PZ[:, e % 2, 0:P + 1], onehot[r, g, :], cum[r, g, 0:P + 1], start=True, stop=True).then_inc(s_find, 1)

            for e in range(AHEAD - PER):
                find(e)

            def gathered_transpose(k):
                e0, n = UNITS[k]
                pe.wait_ge(s_g[k], 16 * n)
                if k >= 1:
                    pe.wait_ge(s_gTs, k)
                for q in range(n):
                    ins = nc.tensor.transpose(PT[:, 0, q * P:(q + 1) * P], xg[:, e0 + q, 0:C], ident)
                ins.then_inc(s_gT, 1)

            def up(k):
                e0, n = UNITS[k]
                pe.wait_ge(s_gTs, k + 1)
                for j, (f0, fn) in enumerate(FF):
                    at = 3 * k + j
                    if at >= 2:
                        pe.wait_ge(s_act, at - 1)
                    dst = PT[0:fn, 1, 0:n * P] if at % 2 == 0 else PM[0:fn, 0, 0:n * P]
                    mm(dst, wup[:, e0 // PER, f0:f0 + fn], xgT[:, k % 2, 0:n * P], start=True, stop=True).then_inc(s_up, 1)

            def down(k):
                e0, n = UNITS[k]
                pe.wait_ge(s_act, 3 * (k + 1))
                for q in range(n):
                    e = e0 + q
                    if e >= 3:
                        pe.wait_ge(s_eo, e - 2)
                    for j in range(3):
                        w = wdn[:, e, j, :] if j < 2 else wdn2[:, e, :]
                        rows_ = P if j < 2 else FR + 1
                        ins = mm(down_bank(e), act[0:rows_, k % 2, j, q * P:(q + 1) * P], w, start=(j == 0), stop=(j == 2))
                    ins.then_inc(s_dn, 1)
                    find(e + AHEAD)

            pe.wait_ge(s_wup, 16)
            pe.wait_ge(s_wdn, 64)
            gathered_transpose(0)
            for e in range(AHEAD - PER, AHEAD):
                find(e)
            for k in range(len(UNITS)):
                up(k)
                if k + 1 in EARLY:
                    gathered_transpose(k + 1)
                down(k)
                if k + 1 not in EARLY and k + 1 < len(UNITS):
                    gathered_transpose(k + 1)
            for g in range(CH):
                pe.wait_ge(s_ys, g + 1)
                if g >= 2:
                    pe.wait_ge(s_yo, g - 1)
                for u in range(TPC):
                    ins = nc.tensor.transpose(PT[:, g % 2, u * P:(u + 1) * P], ysum[:, g * TPC + u, :], ident)
                ins.then_inc(s_yT, 1)


_INS = ["x", "L0_conv_V", "L0_ffn_W_router", "L0_ffn_b_router", "L0_ffn_W_up", "L0_ffn_b_up", "L0_ffn_W_down", "L0_ffn_b_down"]


def kernel(**inputs):
    import concourse.bacc as bacc
    from concourse.bass_utils import run_bass_kernel_spmd as run

    nc = bacc.Bacc("TRN2", target_bir_lowering=False, num_devices=1)
    arrays = {name: np.ascontiguousarray(inputs[name]) for name in _INS}
    arrays["x"] = arrays["x"].reshape(IMAGES, C, PIX)
    arrays["L0_ffn_b_up"] = np.ascontiguousarray(arrays["L0_ffn_b_up"].T)
    arrays.update(zip(("const_f32", "const_f16", "const_counting"), constants()))
    args = [nc.dram_tensor(f"in_{n}", a.shape, mybir.dt.from_np(a.dtype), kind="ExternalInput").ap() for n, a in arrays.items()]
    out = nc.dram_tensor("out_0", (IMAGES, C, PIX), mybir.dt.float32, kind="ExternalOutput").ap()
    metaformer_block(nc, *args, out)
    r = run(nc, [{f"in_{n}": a for n, a in arrays.items()}], core_ids=[0])
    return r.results[0]["out_0"].reshape(IMAGES, C, SIDE, SIDE)
```
